# Optimizing a Trainium2 kernel written in Bass

```python
import numpy as np
import jax
import jax.numpy as jnp

def _softmax(x, axis=-1):
    return jax.nn.softmax(x, axis=axis)

def _gelu(x):
    return jax.nn.gelu(x, approximate=True)

def _silu(x):
    return jax.nn.silu(x)

def _sigmoid(x):
    return jax.nn.sigmoid(x)

def _layernorm(x, axis=-1, eps=1e-05):
    m = jnp.mean(x, axis=axis, keepdims=True)
    v = jnp.var(x, axis=axis, keepdims=True)
    return (x - m) / jnp.sqrt(v + eps)

def _scatter_add(tgt, idx, src, axis=0):
    return tgt.at[idx].add(src)

def _segment_sum(src, seg, n):
    return jax.ops.segment_sum(src, seg, n)
kernel_name = 'mk_prb_d1_jaxref_r8_17d16a'

def setup_inputs(seed: int=0):
    np.random.seed(seed)
    _w = jnp.asarray

    def _L0_attn_setup():
        import jax, jax.numpy as jnp
        import numpy as np
        B, N, H = (2, 512, 256)
        NH, HD = (16, 128)
        BLK = 32
        EPS = 1e-06

        def _lightning_attn(x, slope_rate, w_qkv, w_gate, w_out, norm_w):
            b, n, _ = x.shape
            h, d = (NH, HD)
            nb = n // BLK
            qkv = jax.nn.silu(jnp.einsum('bnf,of->bno', x, w_qkv))
            qkv = qkv.reshape(b, n, h, 3 * d)
            q, k, v = jnp.split(qkv, 3, axis=-1)
            q = q.transpose(0, 2, 1, 3)
            k = k.transpose(0, 2, 1, 3)
            v = v.transpose(0, 2, 1, 3)
            s = slope_rate.astype(jnp.float32)
            arr = jnp.arange(1, BLK + 1, dtype=jnp.float32)
            q_decay = jnp.exp(-s * arr[:, None])
            k_decay = jnp.exp(-s * (BLK - arr)[:, None])
            idx = arr[:, None] - arr[None, :]
            diag_decay = jnp.where(idx >= 0, jnp.exp(-s * idx), 0.0)
            block_decay = jnp.exp(-s * BLK)
            qb = q.reshape(b, h, nb, BLK, d).transpose(2, 0, 1, 3, 4)
            kb = k.reshape(b, h, nb, BLK, d).transpose(2, 0, 1, 3, 4)
            vb = v.reshape(b, h, nb, BLK, d).transpose(2, 0, 1, 3, 4)

            def step(kv, blk):
                qi, ki, vi = blk
                o_inter = jnp.einsum('bhmd,bhde->bhme', qi * q_decay, kv)
                qk = jnp.einsum('bhmd,bhnd->bhmn', qi, ki) * diag_decay
                o_intra = jnp.einsum('bhmn,bhne->bhme', qk, vi)
                kv_new = block_decay * kv + jnp.einsum('bhmd,bhme->bhde', ki * k_decay, vi)
                return (kv_new, o_inter + o_intra)
            kv0 = jnp.zeros((b, h, d, d), dtype=jnp.float32)
            _, out = jax.lax.scan(step, kv0, (qb, kb, vb))
            out = out.transpose(1, 2, 0, 3, 4).reshape(b, h, n, d)
            out = out.transpose(0, 2, 1, 3).reshape(b, n, h * d)
            var = jnp.mean(out * out, axis=-1, keepdims=True)
            out = norm_w * (out * jax.lax.rsqrt(var + EPS))
            gate = jax.nn.sigmoid(jnp.einsum('bnf,of->bno', x, w_gate))
            return jnp.einsum('bno,fo->bnf', gate * out, w_out)
        key = jax.random.key(seed)
        ks = jax.random.split(key, 5)
        scale = 0.02
        x = jax.random.normal(ks[0], (B, N, H), dtype=jnp.float32)
        slopes = (1.0 / 2.0 ** (8.0 * np.arange(1, NH + 1) / NH)).astype(np.float32)
        slope_rate = jnp.asarray(slopes).reshape(NH, 1, 1)
        w_qkv = jax.random.normal(ks[1], (3 * NH * HD, H), dtype=jnp.float32) * scale
        w_gate = jax.random.normal(ks[2], (NH * HD, H), dtype=jnp.float32) * scale
        w_out = jax.random.normal(ks[3], (H, NH * HD), dtype=jnp.float32) * scale
        norm_w = jnp.ones((NH * HD,), dtype=jnp.float32)
        return {'hidden_states': x, 'slope_rate': slope_rate, 'w_qkv': w_qkv, 'w_gate': w_gate, 'w_out': w_out, 'norm_w': norm_w}
    _L0_attn_in = _L0_attn_setup()

    def _L0_ffn_setup():
        import jax, jax.numpy as jnp
        import numpy as np
        B, T, D = (2, 128, 256)
        E, F, K = (64, 64, 4)
        S, HS = (2, 64 * 4)
        key = jax.random.key(seed)
        ks = jax.random.split(key, 9)
        s = 0.02
        f32 = jnp.float32
        return {'x': jax.random.normal(ks[0], (B, T, D), f32), 'router_w': jax.random.normal(ks[1], (D, E), f32) * s, 'router_bias': jnp.zeros((E,), f32), 'wg': jax.random.normal(ks[2], (E, D, F), f32) * s, 'wu': jax.random.normal(ks[3], (E, D, F), f32) * s, 'wd': jax.random.normal(ks[4], (E, F, D), f32) * s, 'swg': jax.random.normal(ks[5], (S, D, HS), f32) * s, 'swu': jax.random.normal(ks[6], (S, D, HS), f32) * s, 'swd': jax.random.normal(ks[7], (S, HS, D), f32) * s}
    _L0_ffn_in = _L0_ffn_setup()
    _d = {'L0_attn_hidden_states': _L0_attn_in['hidden_states'], 'L0_attn_slope_rate': _L0_attn_in['slope_rate'], 'L0_attn_w_qkv': _L0_attn_in['w_qkv'], 'L0_attn_w_gate': _L0_attn_in['w_gate'], 'L0_attn_w_out': _L0_attn_in['w_out'], 'L0_attn_norm_w': _L0_attn_in['norm_w'], 'L0_ffn_router_w': _L0_ffn_in['router_w'], 'L0_ffn_router_bias': _L0_ffn_in['router_bias'], 'L0_ffn_wg': _L0_ffn_in['wg'], 'L0_ffn_wu': _L0_ffn_in['wu'], 'L0_ffn_wd': _L0_ffn_in['wd'], 'L0_ffn_swg': _L0_ffn_in['swg'], 'L0_ffn_swu': _L0_ffn_in['swu'], 'L0_ffn_swd': _L0_ffn_in['swd']}
    _x0 = _d['L0_attn_hidden_states']
    _d['L0_attn_hidden_states'] = jax.random.normal(jax.random.fold_in(jax.random.key(seed), 1), (2, 2048, 256), dtype=_x0.dtype)
    del _x0
    return _d

def reference(L0_attn_hidden_states, L0_attn_slope_rate, L0_attn_w_qkv, L0_attn_w_gate, L0_attn_w_out, L0_attn_norm_w, L0_ffn_router_w, L0_ffn_router_bias, L0_ffn_wg, L0_ffn_wu, L0_ffn_wd, L0_ffn_swg, L0_ffn_swu, L0_ffn_swd):

    def _L0_attn_ref(hidden_states, slope_rate, w_qkv, w_gate, w_out, norm_w):
        import jax, jax.numpy as jnp
        import numpy as np
        B, N, H = (2, 512, 256)
        NH, HD = (16, 128)
        BLK = 32
        EPS = 1e-06

        def _lightning_attn(x, slope_rate, w_qkv, w_gate, w_out, norm_w):
            b, n, _ = x.shape
            h, d = (NH, HD)
            nb = n // BLK
            qkv = jax.nn.silu(jnp.einsum('bnf,of->bno', x, w_qkv))
            qkv = qkv.reshape(b, n, h, 3 * d)
            q, k, v = jnp.split(qkv, 3, axis=-1)
            q = q.transpose(0, 2, 1, 3)
            k = k.transpose(0, 2, 1, 3)
            v = v.transpose(0, 2, 1, 3)
            s = slope_rate.astype(jnp.float32)
            arr = jnp.arange(1, BLK + 1, dtype=jnp.float32)
            q_decay = jnp.exp(-s * arr[:, None])
            k_decay = jnp.exp(-s * (BLK - arr)[:, None])
            idx = arr[:, None] - arr[None, :]
            diag_decay = jnp.where(idx >= 0, jnp.exp(-s * idx), 0.0)
            block_decay = jnp.exp(-s * BLK)
            qb = q.reshape(b, h, nb, BLK, d).transpose(2, 0, 1, 3, 4)
            kb = k.reshape(b, h, nb, BLK, d).transpose(2, 0, 1, 3, 4)
            vb = v.reshape(b, h, nb, BLK, d).transpose(2, 0, 1, 3, 4)

            def step(kv, blk):
                qi, ki, vi = blk
                o_inter = jnp.einsum('bhmd,bhde->bhme', qi * q_decay, kv)
                qk = jnp.einsum('bhmd,bhnd->bhmn', qi, ki) * diag_decay
                o_intra = jnp.einsum('bhmn,bhne->bhme', qk, vi)
                kv_new = block_decay * kv + jnp.einsum('bhmd,bhme->bhde', ki * k_decay, vi)
                return (kv_new, o_inter + o_intra)
            kv0 = jnp.zeros((b, h, d, d), dtype=jnp.float32)
            _, out = jax.lax.scan(step, kv0, (qb, kb, vb))
            out = out.transpose(1, 2, 0, 3, 4).reshape(b, h, n, d)
            out = out.transpose(0, 2, 1, 3).reshape(b, n, h * d)
            var = jnp.mean(out * out, axis=-1, keepdims=True)
            out = norm_w * (out * jax.lax.rsqrt(var + EPS))
            gate = jax.nn.sigmoid(jnp.einsum('bnf,of->bno', x, w_gate))
            return jnp.einsum('bno,fo->bnf', gate * out, w_out)
        return _lightning_attn(hidden_states, slope_rate, w_qkv, w_gate, w_out, norm_w)

    def _L0_ffn_ref(x, router_w, router_bias, wg, wu, wd, swg, swu, swd):
        import jax, jax.numpy as jnp
        import numpy as np
        B, T, D = (2, 128, 256)
        E, F, K = (64, 64, 4)
        S, HS = (2, 64 * 4)
        b, t, d = x.shape
        flat = x.reshape(b * t, d)
        n = flat.shape[0]
        logits = flat @ router_w
        scores = jax.nn.softmax(logits, axis=-1)
        _, topk_idx = jax.lax.top_k(logits + router_bias, K)
        topk_scores = jnp.take_along_axis(scores, topk_idx, axis=-1)
        topk_scores = topk_scores / topk_scores.sum(axis=-1, keepdims=True)
        comb = jnp.zeros((n, E), dtype=flat.dtype).at[jnp.arange(n)[:, None], topk_idx].set(topk_scores)
        g = jax.nn.silu(jnp.einsum('nd,edf->nef', flat, wg))
        u = jnp.einsum('nd,edf->nef', flat, wu)
        routed = jnp.einsum('ne,nef,efd->nd', comb, g * u, wd)
        sg = jax.nn.silu(jnp.einsum('nd,sdh->nsh', flat, swg))
        su = jnp.einsum('nd,sdh->nsh', flat, swu)
        shared = jnp.einsum('nsh,shd->nd', sg * su, swd)
        return (routed + shared).reshape(b, t, d)
    x = L0_attn_hidden_states
    xn = _layernorm(x, axis=-1)
    x = x + _L0_attn_ref(xn, L0_attn_slope_rate, L0_attn_w_qkv, L0_attn_w_gate, L0_attn_w_out, L0_attn_norm_w) + _L0_ffn_ref(xn, L0_ffn_router_w, L0_ffn_router_bias, L0_ffn_wg, L0_ffn_wu, L0_ffn_wd, L0_ffn_swg, L0_ffn_swu, L0_ffn_swd)
    return x

_drawn_inputs = setup_inputs


def setup_inputs(seed=0):
    import zlib

    import numpy as np

    out = dict(_drawn_inputs(seed))
    spreads = {'L0_attn_norm_w': (1.0, 0.6), 'L0_ffn_router_bias': (0.0, 0.8)}
    factors = {'L0_ffn_router_w': 8.0,
     'L0_ffn_wg': 8.0,
     'L0_ffn_wu': 8.0,
     'L0_ffn_wd': 8.0,
     'L0_attn_w_gate': 11.097,
     'L0_ffn_swg': 8.0,
     'L0_ffn_swu': 8.0,
     'L0_ffn_swd': 8.0}
    for name, (base, spread) in spreads.items():
        noise = np.random.default_rng([zlib.crc32(name.encode()), seed]).standard_normal(out[name].shape)
        drawn = base * np.exp(spread * noise) if base else spread * noise
        out[name] = jnp.asarray(drawn.astype(out[name].dtype))
    for name, factor in factors.items():
        out[name] = (out[name] * factor).astype(out[name].dtype)
    return out
```

```python
from contextlib import ExitStack

import concourse.bass as bass
from concourse import mybir

F32 = mybir.dt.float32
F32R = mybir.dt.float32r
BF16 = mybir.dt.bfloat16
I32 = mybir.dt.int32
U32 = mybir.dt.uint32
ALU = mybir.AluOpType
ACT = mybir.ActivationFunctionType
AX = mybir.AxisListType

P = 128
B, N, D = 2, 2048, 256
T = B * N
KD = D // P
NH, HD = 16, 128
SB = 512
NSB = T // SB
CH = SB // P
SB_PER_SEQ = N // SB
NT = T // P
E, F, TOPK = 64, 64, 4
SLOT_TILES = T * TOPK // P + E
S, HS = 2, 256
FT = S * HS // P
LN_EPS = 1e-5
RMS_EPS = 1e-6
NSTEP = NH * NSB
SW = 2 * KD * 512 + FT * D
RING = 4
LINKS = 20
WC = KD * 4 * P
TAB = 2 * P + 2


def lightning_moe(nc, x, slope, wqkv, wgate, wout, norm_w, router_w, router_bias,
                  wgu, wd, swg, swu, swd, out):
    xn_dram = nc.dram_tensor("xn_rows", [T, D], F32, kind="Internal").ap()
    slot_x = nc.dram_tensor("slot_x", [SLOT_TILES * P, D], F32, kind="Internal").ap()
    slot_y = nc.dram_tensor("slot_y", [SLOT_TILES * P, D], F32, kind="Internal").ap()

    top = ExitStack()
    with top:
        def sem(name):
            return top.enter_context(nc.semaphore(name))

        def sb_in(stack):
            return lambda name, shape, dt=F32: stack.enter_context(nc.sbuf_tensor(name, shape, dt))

        bank = [top.enter_context(nc.psum_tensor(f"bank{i}", [P, 512], F32)) for i in range(8)]
        keep = sb_in(top)
        xh = keep("xh", [P, KD, T], F32R)
        xl = keep("xl", [P, KD, T], F32R)
        ident = keep("ident", [P, P])
        ones = keep("ones", [P, 1])
        pos = keep("pos", [P, NT, TOPK], U32)
        wgt = keep("wgt", [P, NT, TOPK])
        etab = keep("etab", [1, 2 * P], I32)
        tab = keep("tab", [P, NH, TAB])
        raw = keep("raw", [P, WC + D + 1])

        rms = keep("rms", [P, NT])
        rmsv = keep("rmsv", [P, NT])
        mhalf2 = keep("mhalf2", [P, NT])
        zeros = keep("zeros", [P, 2 * D])

        with ExitStack() as st:
            sb = sb_in(st)
            xin = [sb(f"xin{i}", [P, CH, D]) for i in range(2)]
            xn = [sb(f"xn{i}", [P, CH, D]) for i in range(2)]
            xf = sb("xf", [P, KD, SB])
            rw = sb("rw", [P, KD, E])
            rbias = sb("rbias", [P, E])
            stat = sb("stat", [P, CH, 6])
            mv = sb("mv", [P, CH, 2])
            ve = sb("ve", [P, CH])
            rs = sb("rs", [P, CH])
            mhalf = sb("mhalf", [P, CH])
            upper = sb("upper", [P, P], BF16)
            ones_bf = sb("ones_bf", [P, P], BF16)
            iota_e = sb("iota_e", [P, E])
            lgb = sb("lgb", [P, CH, E])
            m8 = sb("m8", [P, CH, 8])
            i8 = sb("i8", [P, CH, 8], U32)
            idxf = sb("idxf", [P, CH * TOPK])
            mx = sb("mx", [P, CH])
            lc = sb("lc", [P, CH, E])
            pr = sb("pr", [P, CH, E])
            z = sb("z", [P, CH])
            zi = sb("zi", [P, CH])
            oh = sb("oh", [P, NT * TOPK, E], BF16)
            prod = sb("prod", [P, CH * TOPK, E])
            pk = sb("pk", [P, CH, TOPK])
            pz = sb("pz", [P, CH, TOPK])
            ps4 = sb("ps4", [P, CH])
            pi4 = sb("pi4", [P, CH])
            mask = sb("mask", [P, CH, E], BF16)
            mgrp = sb("mgrp", [P, E])
            macc = sb("macc", [P, E], BF16)
            rank = sb("rank", [P, NT * TOPK])
            posf = sb("posf", [P, NT * TOPK])
            tot_i = sb("tot_i", [P, E], I32)
            tot_a = sb("tot_a", [P, E], I32)
            tot_s = sb("tot_s", [P, E], I32)
            cnt = sb("cnt", [P, E])
            incl = sb("incl", [P, E])
            base = sb("base", [P, E])
            base2 = sb("base2", [P, E])
            zero_e = sb("zero_e", [P, E])
            tcol = sb("tcol", [P, 2])
            le = sb("le", [P, 2, E])
            ecol = sb("ecol", [P, 2])
            ecl = sb("ecl", [P, 2])
            nslope = sb("nslope", [P, NH])
            slope_b = sb("slope_b", [P, NH])
            ns_all = sb("ns_all", [P, NH])
            dm = sb("dm", [P, P])
            dm0 = sb("dm0", [P, P])
            mrow = sb("mrow", [P, P])
            kcol = sb("kcol", [P, NH])
            karg = sb("karg", [P, NH])

        acc = keep("acc", [P, KD, T])
        ssq = keep("ssq", [P, T])
        with ExitStack() as st:
            sb = sb_in(st)
            wh = [sb(f"wh{i}", [P, WC + D], F32R) for i in range(2)]
            wl = [sb(f"wl{i}", [P, WC + D], F32R) for i in range(2)]
            row = sb("row", [P, CH, D])
            cur_pos = [sb(f"cur_pos{r}", [P, TOPK], U32) for r in range(CH)]
            wos = sb("wos", [P, D])
            hc = [sb(f"hc{i}", [P, TAB]) for i in range(2)]
            kT = sb("kT", [P, SB])
            vT = sb("vT", [P, SB])
            qT = sb("qT", [P, SB])
            tg = sb("tg", [P, SB])
            kp = sb("kp", [P, SB])
            vt = sb("vt", [P, SB])
            sm = sb("sm", [P, SB])
            qp = sb("qp", [P, SB])
            o2 = sb("o2", [P, SB])
            og = sb("og", [P, SB])
            ogh = sb("ogh", [P, SB], F32R)
            ogl = sb("ogl", [P, SB], F32R)
            state = sb("state", [P, CH, HD])

        swh = keep("swh", [P, SW], F32R)
        swl = keep("swl", [P, SW], F32R)
        with ExitStack() as st:
            sb = sb_in(st)
            sraw = sb("sraw", [P, SW])
            xs = [sb(f"xs{i}", [P, D]) for i in range(RING)]
            gu = [sb(f"gu{i}", [P, KD, 2 * F]) for i in range(RING)]
            wde = [sb(f"wde{i}", [F, D]) for i in range(RING)]
            xsT = [sb(f"xsT{i}", [P, KD, P]) for i in range(2)]
            sg = [sb(f"sg{i}", [P, F]) for i in range(2)]
            he = [sb(f"he{i}", [P, F]) for i in range(2)]
            hT = [sb(f"hT{i}", [F, P]) for i in range(2)]
            ys = [sb(f"ys{i}", [P, D]) for i in range(RING)]
        with ExitStack() as st:
            sb = sb_in(st)
            ssg = [sb(f"ssg{i}", [P, SB]) for i in range(2)]
            sh = [sb(f"sh{i}", [P, SB]) for i in range(2)]
            shh = sb("shh", [P, FT, SB], F32R)
            shl = sb("shl", [P, FT, SB], F32R)
            accs = sb("accs", [P, KD, SB])
            xr = [sb(f"xr{i}", [P, D]) for i in range(2)]
            yk = [sb(f"yk{i}", [P, TOPK, D]) for i in range(2)]
            res = [sb(f"res{i}", [P, D]) for i in range(2)]
            cols = [sb(f"cols{i}", [P, 1 + TOPK]) for i in range(2)]
            picked = [sb(f"picked{i}", [P, TOPK], U32) for i in range(2)]

        consts_loaded = sem("consts_loaded")
        pool_step = sem("pool_step")
        dve_const = sem("dve_const")
        tables = sem("tables")
        tab_ready = sem("tab_ready")
        x_loaded = [sem(f"x_loaded{u}") for u in range(2)]
        slots_zero = sem("slots_zero")
        stats_done = sem("stats_done")
        aggr_done = sem("aggr_done")
        var_ready = sem("var_ready")
        rstd_ready = sem("rstd_ready")
        xn_ready = sem("xn_ready")
        xn_stored = [sem(f"xn_stored{u}") for u in range(2)]
        xT_mm = sem("xT_mm")
        xf_ready = sem("xf_ready")
        xh_ready = sem("xh_ready")
        xl_ready = sem("xl_ready")
        logits_mm = sem("logits_mm")
        route = sem("route")
        lc_ready = sem("lc_ready")
        pr_ready = sem("pr_ready")
        mask_ready = sem("mask_ready")
        rank_mm = sem("rank_mm")
        macc_ready = sem("macc_ready")
        tot_mm = sem("tot_mm")
        etab_mm = sem("etab_mm")
        ecl_ready = sem("ecl_ready")
        routed = sem("routed")
        raw_loaded = sem("raw_loaded")
        wos_ready = sem("wos_ready")
        wh_ready = sem("wh_ready")
        w_ready = sem("w_ready")
        zeroed = sem("zeroed")
        k_mm = sem("k_mm")
        v_mm = sem("v_mm")
        q_mm = sem("q_mm")
        kT_mm = sem("kT_mm")
        vT_mm = sem("vT_mm")
        g_mm = sem("g_mm")
        s_mm = sem("s_mm")
        kv_mm = sem("kv_mm")
        out_mm = sem("out_mm")
        o_mm = sem("o_mm")
        k_silu = sem("k_silu")
        v_silu = sem("v_silu")
        q_silu = sem("q_silu")
        vt_ready = sem("vt_ready")
        tanh_done = sem("tanh_done")
        o2_ready = sem("o2_ready")
        ogh_ready = sem("ogh_ready")
        ogl_ready = sem("ogl_ready")
        qp_ready = sem("qp_ready")
        kp_ready = sem("kp_ready")
        sm_ready = sem("sm_ready")
        state_step = sem("state_step")
        state_zero = sem("state_zero")
        acc_added = sem("acc_added")
        og_ready = sem("og_ready")
        ssq_added = sem("ssq_added")
        row_loaded = [sem(f"row_loaded{r}") for r in range(CH)]
        idx_copied = sem("idx_copied")
        scattered = [sem(f"scattered{r}") for r in range(CH)]
        rms_mm = sem("rms_mm")
        rmsv_ready = sem("rmsv_ready")
        rms_ready = sem("rms_ready")
        sraw_loaded = sem("sraw_loaded")
        swh_ready = sem("swh_ready")
        swl_ready = sem("swl_ready")
        tile_loaded = [sem(f"tile_loaded{r}") for r in range(RING)]
        xsT_mm = sem("xsT_mm")
        xsT_ready = sem("xsT_ready")
        gu_mm = sem("gu_mm")
        sg_ready = sem("sg_ready")
        he_ready = sem("he_ready")
        hT_mm = sem("hT_mm")
        hT_ready = sem("hT_ready")
        y_mm = sem("y_mm")
        ys_ready = sem("ys_ready")
        y_stored = [sem(f"y_stored{r}") for r in range(RING)]
        sgu_mm = sem("sgu_mm")
        ssg_ready = sem("ssg_ready")
        sh_ready = sem("sh_ready")
        shh_ready = sem("shh_ready")
        shl_ready = sem("shl_ready")
        accs_ready = sem("accs_ready")
        accT_mm = sem("accT_mm")
        down_mm = sem("down_mm")
        cols_ready = sem("cols_ready")
        xr_loaded = [sem(f"xr_loaded{r}") for r in range(2)]
        picked_ready = sem("picked_ready")
        gathered = [sem(f"gathered{r}") for r in range(2)]
        summed = sem("summed")
        out_stored = [sem(f"out_stored{r}") for r in range(2)]

        x_grp = x.rearrange("(g c p) d -> g p c d", c=CH, p=P)
        xn_grp = xn_dram.rearrange("(g c p) d -> g p c d", c=CH, p=P)
        x_tile = x.rearrange("(t p) d -> t p d", p=P)
        xn_tile = xn_dram.rearrange("(t p) d -> t p d", p=P)
        out_tile = out.rearrange("(t p) d -> t p d", p=P)
        slot_x_tile = slot_x.rearrange("(t p) d -> t p d", p=P)
        slot_y_tile = slot_y.rearrange("(t p) d -> t p d", p=P)
        zero_parts = slot_x.rearrange("(q p n r) d -> q p n (r d)", q=4, p=P, r=2)

        def at(ap, i):
            letters = "abcd"[:len(ap.shape) - 1]
            names = " ".join(letters)
            return ap[bass.ds(i, 1)].rearrange(f"o {letters[0]} {' '.join(letters[1:])} -> (o {letters[0]}) {' '.join(letters[1:])}")

        def at_col(tensor, i):
            if len(tensor.shape) == 2:
                return tensor[:, bass.ds(i, 1)]
            return tensor[:, bass.ds(i, 1), :].rearrange("p o n -> p (o n)")

        def chunks(ap):
            return ap.rearrange("p (c m) -> p c m", c=CH)

        def per_chunk(ap):
            return ap.unsqueeze(1).to_broadcast([P, CH, ap.shape[-1]])

        block = top.enter_context(nc.Block())

        @block.sync
        def _(sp):
            for dst, src in ((rw[:], router_w.rearrange("(k p) e -> p k e", p=P)),
                             (rbias[:], router_bias.partition_broadcast(P)),
                             (slope_b[:], slope.partition_broadcast(P))):
                sp.dma_start(dst, src).then_inc(consts_loaded, 16)

            with sp.Fori(0, NSB // 2) as g2:
                for u in range(2):
                    sp.wait_ge(xn_ready, CH * 2 * g2)
                    sp.dma_start(xin[u][:], at(x_grp, g2 * 2 + u)).then_inc(x_loaded[u], 16)
                for u in range(2):
                    sp.wait_ge(xn_ready, CH * (2 * g2 + u + 1))
                    sp.dma_start(at(xn_grp, g2 * 2 + u), xn[u][:]).then_inc(xn_stored[u], 16)
            sp.wait_ge(dve_const, 1)
            for q in range(4):
                sp.dma_start(zero_parts[q], zeros[:].unsqueeze(1).to_broadcast([P, SLOT_TILES // 8, 2 * D])).then_inc(slots_zero, 16)

            def load_head(h):
                w = raw[:, 0:WC].rearrange("p (k n) -> p k n", k=KD)
                sp.dma_start(w[:, :, 0:3 * HD], at(wqkv, h)).then_inc(raw_loaded, 16)
                sp.dma_start(w[:, :, 3 * HD:4 * HD], at(wgate, h)).then_inc(raw_loaded, 16)
                sp.dma_start(raw[:, WC:WC + D], at(wout, h)).then_inc(raw_loaded, 16)
                sp.dma_start(raw[:, WC + D:WC + D + 1], at(norm_w, h)).then_inc(raw_loaded, 16)

            load_head(0)
            with sp.Fori(0, NH // 2) as hp:
                for par in range(2):
                    sp.wait_ge(w_ready, 2 * hp + par + 1)
                    load_head(2 * hp + 1 if par == 0 else (2 * hp + 2) % NH)

            sp.wait_ge(acc_added, 2 * (NSTEP + 1))
            sp.wait_ge(ssq_added, NSTEP)
            sp.wait_ge(w_ready, NH + 1)
            for r in range(CH):
                sp.wait_ge(scattered[r], 16 * TOPK * NT // CH)
            w = sraw[:, 0:2 * KD * 512].rearrange("p (i k s h) -> p i k s h", i=2, k=KD, s=S)
            for i, src in enumerate((swg, swu)):
                for s in range(S):
                    sp.dma_start(w[:, i, :, s, :], src[s].rearrange("(k p) h -> p k h", p=P)).then_inc(sraw_loaded, 16)
            sp.dma_start(sraw[:, 2 * KD * 512:].rearrange("p (t d) -> p t d", d=D),
                         swd.rearrange("s (t p) d -> p (s t) d", p=P)).then_inc(sraw_loaded, 16)

            def load_tile(t, r):
                e = sp.value_load(etab[0:1, bass.ds(t, 1)], min_val=0, max_val=E - 1)
                sp.dma_start(xs[r][:], at(slot_x_tile, t)).then_inc(tile_loaded[r], 16)
                sp.dma_start(gu[r][:], at(wgu, e)).then_inc(tile_loaded[r], 16)
                sp.dma_start(wde[r][:], at(wd, e)).then_inc(tile_loaded[r], 16)

            def store_tile(t, r):
                sp.wait_ge(ys_ready, t + 1)
                sp.dma_start(at(slot_y_tile, t), ys[r][:]).then_inc(y_stored[r], 16)

            for r in range(RING):
                load_tile(r, r)
            with sp.Fori(0, SLOT_TILES // RING - 1) as q:
                for r in range(RING):
                    store_tile(q * RING + r, r)
                    load_tile(q * RING + RING + r, r)
            for r in range(RING):
                store_tile(SLOT_TILES - RING + r, r)

            for r in range(RING):
                sp.wait_ge(y_stored[r], 16 * SLOT_TILES // RING)
            sp.wait_ge(xsT_ready, SLOT_TILES)
            with sp.Fori(0, NT // 2) as t2:
                for r in range(2):
                    sp.wait_ge(summed, 6 * 2 * t2)
                    sp.dma_start(xr[r][:], at(x_tile, t2 * 2 + r)).then_inc(xr_loaded[r], 16)
                for r in range(2):
                    sp.wait_ge(summed, 6 * (2 * t2 + r + 1))
                    sp.dma_start(at(out_tile, t2 * 2 + r), res[r][:]).then_inc(out_stored[r], 16)
            for r in range(2):
                sp.wait_ge(out_stored[r], 16 * NT // 2)

        @block.gpsimd
        def _(pool):
            pool.memset(ident[:], 0.0).then_inc(pool_step, 1)
            pool.memset(upper[:], 1.0).then_inc(pool_step, 1)
            pool.iota(dm[:], [[1, P]], base=0, channel_multiplier=-1, allow_small_or_imprecise_dtypes=True).then_inc(pool_step, 1)
            pool.iota(mrow[:], [[1, P]], base=1, channel_multiplier=0, allow_small_or_imprecise_dtypes=True).then_inc(pool_step, 1)
            pool.iota(kcol[:], [[0, NH]], base=P - 1, channel_multiplier=-1, allow_small_or_imprecise_dtypes=True).then_inc(pool_step, 1)
            pool.iota(iota_e[:], [[1, E]], base=0, channel_multiplier=0, allow_small_or_imprecise_dtypes=True).then_inc(pool_step, 1)
            pool.iota(tcol[:], [[P, 2]], base=0, channel_multiplier=1, allow_small_or_imprecise_dtypes=True).then_inc(pool_step, 1)
            pool.wait_ge(pool_step, 7)
            pool.affine_select(out=ident[:], in_=ident[:], pattern=[[-1, P]], compare_op=ALU.not_equal, fill=1.0,
                               base=0, channel_multiplier=1).then_inc(pool_step, 1)
            pool.affine_select(out=upper[:], in_=upper[:], pattern=[[1, P]], compare_op=ALU.is_gt, fill=0.0,
                               base=0, channel_multiplier=-1).then_inc(pool_step, 1)
            pool.wait_ge(tables, 2 * NH)
            pool.affine_select(out=tab[:, :, 0:P], in_=tab[:, :, 0:P], pattern=[[0, NH], [1, P]], compare_op=ALU.is_ge,
                               fill=0.0, base=0, channel_multiplier=-1).then_inc(tab_ready, 1)
            pool.wait_ge(dve_const, 2)
            with pool.Fori(0, NSB) as g:
                pool.wait_ge(var_ready, g + 1)
                pool.tensor_tensor(rs[:], ve[:], mhalf[:], ALU.pow).then_inc(rstd_ready, 1)

            pool.wait_ge(routed, 2)
            for u in range(2):
                pool.wait_ge(xn_stored[u], 16 * NSB // 2)
            pool.memset(acc[:], 0.0).then_inc(zeroed, 1)
            pool.memset(ssq[:], 0.0).then_inc(zeroed, 1)
            pool.memset(wh[1][:, WC:WC + D].bitcast(F32), 0.0).then_inc(zeroed, 1)
            pool.memset(wl[1][:, WC:WC + D].bitcast(F32), 0.0).then_inc(zeroed, 1)
            pool.memset(ogh[:].bitcast(F32), 0.0).then_inc(zeroed, 1)
            pool.memset(ogl[:].bitcast(F32), 0.0).then_inc(zeroed, 1)

            pool.wait_ge(slots_zero, 64)
            with pool.Fori(0, NT // CH) as q:
                for r in range(CH):
                    t = q * CH + r
                    pool.wait_ge(scattered[r], 16 * TOPK * q)
                    pool.nop(nofuse=True)
                    pool.tensor_copy(cur_pos[r][:], at_col(pos, t)).then_inc(idx_copied, 1)
                    pool.dma_start(row[:, r, :], at(xn_tile, t)).then_inc(row_loaded[r], 16)
                    pool.wait_ge(idx_copied, t + 1)
                    pool.wait_ge(row_loaded[r], 16 * (q + 1))
                    pool.nop(nofuse=True)
                    for k in range(TOPK):
                        pool.indirect_dma_start(out=slot_x, out_offset=bass.IndirectOffsetOnAxis(cur_pos[r][:, k:k + 1], 0),
                                                in_=row[:, r, :], in_offset=None).then_inc(scattered[r], 16)

            pool.wait_ge(rmsv_ready, 1)
            pool.tensor_tensor(rms[:], rmsv[:], mhalf2[:], ALU.pow).then_inc(rms_ready, 1)

            for r in range(RING):
                pool.wait_ge(y_stored[r], 16 * SLOT_TILES // RING)
            with pool.Fori(0, NT // 2) as q:
                for r in range(2):
                    t = q * 2 + r
                    pool.wait_ge(summed, 6 * 2 * q + 6 * r)
                    pool.nop(nofuse=True)
                    pool.tensor_copy(picked[r][:], at_col(pos, t)).then_inc(picked_ready, 1)
                    pool.wait_ge(picked_ready, t + 1)
                    pool.nop(nofuse=True)
                    for k in range(TOPK):
                        pool.indirect_dma_start(out=yk[r][:, k, :], out_offset=None, in_=slot_y,
                                                in_offset=bass.IndirectOffsetOnAxis(picked[r][:, k:k + 1], 0)).then_inc(gathered[r], 16)

        @block.scalar
        def _(act):
            act.wait_ge(dve_const, 2)
            for h in range(NH):
                act.activation(tab[:, h, 0:P], dm0[:], ACT.Exp, scale=ns_all[:, h:h + 1]).then_inc(tables, 1)
                act.activation(tab[:, h, P:2 * P], mrow[:], ACT.Exp, scale=ns_all[:, h:h + 1]).then_inc(tables, 1)
            act.activation(tab[:, :, 2 * P], karg[:], ACT.Exp).then_inc(tab_ready, 1)
            act.activation(tab[:, :, 2 * P + 1], ns_all[:], ACT.Exp, scale=float(P)).then_inc(tab_ready, 1)

            with act.Fori(0, NSB) as g:
                act.wait_ge(xT_mm, g + 1)
                act.wait_ge(logits_mm, g)
                for k in range(KD):
                    act.copy(xf[:, k, :], bank[k][:]).then_inc(xf_ready, 1)
                act.nop(nofuse=True)
                for k in range(KD):
                    act.copy(xh[:, k, bass.ds(g * SB, SB)], bank[k][:]).then_inc(xh_ready, 1)
                act.wait_ge(lc_ready, g + 1)
                act.activation(pr[:].rearrange("p c e -> p (c e)"), lc[:].rearrange("p c e -> p (c e)"), ACT.Exp).then_inc(pr_ready, 1)

            def split_high(h, par):
                act.wait_ge(raw_loaded, 64 * (h + 1))
                act.copy(wh[par][:, 0:WC], raw[:, 0:WC]).then_inc(wh_ready, 1)
                act.wait_ge(wos_ready, h + 1)
                act.copy(wh[par][:, WC:WC + D], wos[:]).then_inc(wh_ready, 1)

            def step(i):
                act.wait_ge(k_mm, i + 1)
                act.activation(kT[:], bank[0][:], ACT.Silu).then_inc(k_silu, 1)
                act.wait_ge(v_mm, i + 1)
                act.activation(vT[:], bank[1][:], ACT.Silu).then_inc(v_silu, 1)
                act.wait_ge(q_mm, i + 1)
                act.activation(qT[:], bank[2][:], ACT.Silu).then_inc(q_silu, 1)
                act.wait_ge(vT_mm, i + 1)
                act.copy(vt[:], bank[4][:]).then_inc(vt_ready, 1)
                act.wait_ge(g_mm, i + 1)
                act.wait_ge(og_ready, i)
                act.activation(tg[:], bank[0][:], ACT.Tanh, scale=0.5).then_inc(tanh_done, 1)
                act.wait_ge(o_mm, i + 1)
                act.wait_ge(ssq_added, i)
                act.activation(o2[:], bank[5][:], ACT.Square).then_inc(o2_ready, 1)
                act.wait_ge(og_ready, i + 1)
                act.copy(ogh[:], og[:]).then_inc(ogh_ready, 1)

            act.wait_ge(routed, 2)
            act.wait_ge(zeroed, 6)
            split_high(0, 0)
            with act.Fori(0, NH // 2) as hp:
                for par in range(2):
                    h = 2 * hp + par
                    step(h * NSB)
                    act.wait_ge(out_mm, h * NSB + 1)
                    split_high(h + 1, 1 - par)
                    with act.Fori(1, NSB) as b:
                        step(h * NSB + b)

            act.wait_ge(sraw_loaded, 80)
            act.wait_ge(out_mm, NSTEP + 1)
            act.copy(swh[:], sraw[:]).then_inc(swh_ready, 1)

            def transposed(t, u):
                act.wait_ge(xsT_mm, t + 1)
                act.copy(xsT[u][:].rearrange("p k m -> p (k m)"), bank[u][:, 0:D]).then_inc(xsT_ready, 1)

            def silu_tile(t, u):
                act.wait_ge(gu_mm, t + 1)
                act.activation(sg[u][:], bank[2 + u][:, 0:F], ACT.Silu).then_inc(sg_ready, 1)

            transposed(0, 0)
            with act.Fori(0, SLOT_TILES // 2 - 1) as q:
                for r in range(2):
                    transposed(q * 2 + r + 1, 1 - r)
                    silu_tile(q * 2 + r, r)
            transposed(SLOT_TILES - 1, 1)
            silu_tile(SLOT_TILES - 2, 0)
            silu_tile(SLOT_TILES - 1, 1)

            for r in range(RING):
                act.wait_ge(y_stored[r], 16 * SLOT_TILES // RING)
            act.wait_ge(hT_ready, SLOT_TILES)
            with act.Fori(0, NSB) as b:
                act.wait_ge(accT_mm, b)
                act.nop(nofuse=True)
                for k in range(KD):
                    act.copy(accs[:, k, :], acc[:, k, bass.ds(b * SB, SB)]).then_inc(accs_ready, 1)
                for ft in range(FT):
                    j = b * FT + ft
                    act.wait_ge(sgu_mm, j + 1)
                    act.activation(ssg[ft % 2][:], bank[ft % 2][:], ACT.Silu).then_inc(ssg_ready, 1)
                    act.wait_ge(sh_ready, j + 1)
                    if ft == 0:
                        act.wait_ge(down_mm, b)
                    act.copy(shh[:, ft, :], sh[ft % 2][:]).then_inc(shh_ready, 1)

        @block.vector
        def _(dve):
            dve.memset(zeros[:], 0.0).then_inc(dve_const, 1)
            for ap, value in ((ones[:], 1.0), (ones_bf[:], 1.0), (mhalf[:], -0.5), (mhalf2[:], -0.5),
                              (zero_e[:], 0.0)):
                dve.memset(ap, value)
            dve.memset(macc[:], 0.0).then_inc(macc_ready, 1)
            dve.wait_ge(consts_loaded, 48)
            dve.wait_ge(pool_step, 7)
            dve.tensor_scalar(ns_all[:], slope_b[:], -1.0, None, ALU.mult).then_inc(route, 1)
            dve.tensor_scalar(dm0[:], dm[:], 0.0, None, ALU.max).then_inc(route, 1)
            dve.wait_ge(route, 2)
            dve.tensor_tensor(karg[:], kcol[:], ns_all[:], ALU.mult).then_inc(dve_const, 1)
            NCONST = 2

            with dve.Fori(0, NSB // 2) as g2:
                for u in range(2):
                    g = g2 * 2 + u
                    n = [0]

                    def link(ins):
                        n[0] += 1
                        ins.then_inc(route, 1)
                        dve.wait_ge(route, NCONST + g * LINKS + n[0])

                    dve.wait_ge(x_loaded[u], 16 * (g2 + 1))
                    for c in range(CH):
                        dve.bn_stats(stat[:, c, :], xin[u][:, c, :]).then_inc(stats_done, 1)
                    dve.wait_ge(stats_done, CH * (g + 1))
                    dve.nop(nofuse=True)
                    for c in range(CH):
                        dve.bn_aggr(mv[:, c, :], stat[:, c, :]).then_inc(aggr_done, 1)
                    dve.wait_ge(aggr_done, CH * (g + 1))
                    dve.tensor_scalar(ve[:], mv[:, :, 1], LN_EPS, None, ALU.add).then_inc(var_ready, 1)
                    dve.wait_ge(rstd_ready, g + 1)
                    dve.wait_ge(xn_stored[u], 16 * g2)
                    for c in range(CH):
                        dve.tensor_scalar(xn[u][:, c, :], xin[u][:, c, :], mv[:, c, 0:1], rs[:, c:c + 1],
                                          ALU.subtract, ALU.mult).then_inc(xn_ready, 1)
                    dve.wait_ge(xh_ready, KD * (g + 1))
                    for k in range(KD):
                        dve.tensor_tensor(xl[:, k, bass.ds(g * SB, SB)], bank[k][:],
                                          xh[:, k, bass.ds(g * SB, SB)].bitcast(F32), ALU.subtract).then_inc(xl_ready, 1)
                    dve.wait_ge(logits_mm, g + 1)
                    lg = bank[2][:, 0:CH * E].rearrange("p (c e) -> p c e", c=CH)
                    link(dve.tensor_tensor(lgb[:], lg, per_chunk(rbias[:]), ALU.add))
                    link(dve.tensor_reduce(mx[:], lg, AX.X, ALU.max))
                    link(dve.tensor_tensor(lc[:], lg, mx[:].unsqueeze(2).to_broadcast([P, CH, E]), ALU.subtract))
                    dve.sem_inc(lc_ready, 1)
                    for c in range(CH):
                        ins = dve.max(m8[:, c, :], lgb[:, c, :])
                        link(ins) if c == CH - 1 else None
                    dve.nop(nofuse=True)
                    for c in range(CH):
                        ins = dve.max_index(i8[:, c, :], m8[:, c, :], lgb[:, c, :])
                        link(ins) if c == CH - 1 else None
                    link(dve.tensor_copy(idxf[:].rearrange("p (c k) -> p c k", c=CH), i8[:, :, 0:TOPK]))
                    ohg = oh[:, bass.ds(g * CH * TOPK, CH * TOPK), :]
                    link(dve.tensor_tensor(ohg, iota_e[:].unsqueeze(1).to_broadcast([P, CH * TOPK, E]),
                                           idxf[:].unsqueeze(2).to_broadcast([P, CH * TOPK, E]), ALU.is_equal))
                    dve.nop(nofuse=True)
                    with nc.allow_low_precision(reason="counts below 256 are exact"):
                        link(dve.tensor_reduce(mask[:], ohg.rearrange("p (c k) e -> p c e k", k=TOPK), AX.X, ALU.add))
                    dve.sem_inc(mask_ready, 1)
                    dve.wait_ge(pr_ready, g + 1)
                    link(dve.tensor_reduce(z[:], pr[:], AX.X, ALU.add))
                    link(dve.reciprocal(zi[:], z[:]))
                    prod4 = prod[:].rearrange("p (c k) e -> p c k e", k=TOPK)
                    ohg4 = ohg.rearrange("p (c k) e -> p c k e", k=TOPK)
                    link(dve.tensor_tensor(prod4, ohg4, pr[:].unsqueeze(2).to_broadcast([P, CH, TOPK, E]), ALU.mult))
                    link(dve.tensor_reduce(pk[:].rearrange("p c k -> p (c k)"), prod[:], AX.X, ALU.add))
                    link(dve.tensor_tensor(pz[:], pk[:], zi[:].unsqueeze(2).to_broadcast([P, CH, TOPK]), ALU.mult))
                    link(dve.tensor_reduce(ps4[:], pz[:], AX.X, ALU.add))
                    link(dve.reciprocal(pi4[:], ps4[:]))
                    link(dve.tensor_tensor(wgt[:, bass.ds(g * CH, CH), :], pz[:], pi4[:].unsqueeze(2).to_broadcast([P, CH, TOPK]), ALU.mult))
                    dve.wait_ge(rank_mm, g + 1)
                    rk = bank[3][:, 0:CH * E].rearrange("p (c e) -> p c e", c=CH)
                    link(dve.tensor_tensor(prod4, ohg4, rk.unsqueeze(2).to_broadcast([P, CH, TOPK, E]), ALU.mult))
                    dve.nop(nofuse=True)
                    link(dve.tensor_reduce(rank[:, bass.ds(g * CH * TOPK, CH * TOPK)], prod[:], AX.X, ALU.add))
                    link(dve.tensor_reduce(mgrp[:], mask[:].rearrange("p c e -> p e c"), AX.X, ALU.add))
                    link(dve.tensor_tensor(macc[:], macc[:], mgrp[:], ALU.add))
                    dve.sem_inc(macc_ready, 1)
                    assert n[0] == LINKS, n

            done = [NCONST + NSB * LINKS]

            def link(ins):
                done[0] += 1
                ins.then_inc(route, 1)
                dve.wait_ge(route, done[0])

            dve.wait_ge(tot_mm, 1)
            link(dve.tensor_scalar(tot_a[:], bank[4][:, 0:E], float(P - 1), None, ALU.add))
            link(dve.tensor_single_scalar(tot_s[:], tot_a[:], P.bit_length() - 1, ALU.logical_shift_right))
            link(dve.tensor_copy(cnt[:], tot_s[:]))
            link(dve.tensor_tensor_scan(incl[:], cnt[:], zero_e[:], 0.0, ALU.add, ALU.add))
            link(dve.tensor_tensor(base[:], incl[:], cnt[:], ALU.subtract))
            link(dve.tensor_scalar(base2[:], base[:], float(P), None, ALU.mult))
            for g in range(NSB):
                s = slice(g * CH * TOPK, (g + 1) * CH * TOPK)
                link(dve.tensor_tensor(prod[:], oh[:, s, :], base2[:].unsqueeze(1).to_broadcast([P, CH * TOPK, E]), ALU.mult))
                link(dve.tensor_reduce(posf[:, s], prod[:], AX.X, ALU.add))
            dve.tensor_tensor(pos[:].rearrange("p t k -> p (t k)"), posf[:], rank[:], ALU.add).then_inc(routed, 1)
            for j in range(2):
                link(dve.tensor_scalar(le[:, j, :], incl[:], tcol[:, j:j + 1], None, ALU.is_le))
            link(dve.tensor_reduce(ecol[:], le[:], AX.X, ALU.add))
            dve.tensor_scalar(ecl[:], ecol[:], float(E - 1), None, ALU.min).then_inc(ecl_ready, 1)
            dve.wait_ge(etab_mm, 1)
            dve.tensor_copy(etab[:], bank[5][0:1, 0:2 * P]).then_inc(routed, 1)

            def split_low(h, par):
                dve.wait_ge(raw_loaded, 64 * (h + 1))
                dve.tensor_scalar(wos[:], raw[:, WC:WC + D], raw[:, WC + D:WC + D + 1], 0.5,
                                  ALU.mult, ALU.mult).then_inc(wos_ready, 1)
                dve.wait_ge(wh_ready, 2 * (h + 1))
                dve.tensor_tensor(wl[par][:, 0:WC], raw[:, 0:WC], wh[par][:, 0:WC].bitcast(F32), ALU.subtract)
                dve.tensor_tensor(wl[par][:, WC:WC + D], wos[:], wh[par][:, WC:WC + D].bitcast(F32), ALU.subtract)

            def head_tables(h, par):
                dve.tensor_copy(hc[par][:], at_col(tab, h)).then_inc(w_ready, 1)

            def step(i, b_prev, par, first):
                dkT = per_chunk(hc[par][:, 0:P])
                qd = per_chunk(hc[par][:, P:2 * P])
                kd, bd = hc[par][:, 2 * P:2 * P + 1], hc[par][:, 2 * P + 1:2 * P + 2]
                if first:
                    dve.wait_ge(state_step, 4 * i)
                    dve.memset(state[:, 0, :], 0.0).then_inc(state_zero, 1)
                dve.wait_ge(q_silu, i + 1)
                dve.tensor_tensor(chunks(qp[:]), chunks(qT[:]), qd, ALU.mult).then_inc(qp_ready, 1)
                dve.wait_ge(kT_mm, i + 1)
                dve.tensor_scalar(kp[:], bank[3][:], kd, None, ALU.mult).then_inc(kp_ready, 1)
                dve.wait_ge(s_mm, i + 1)
                dve.tensor_tensor(chunks(sm[:]), chunks(bank[1][:]), dkT, ALU.mult).then_inc(sm_ready, 1)
                dve.wait_ge(kv_mm, i + 1)
                if first:
                    dve.wait_ge(state_zero, first(i))
                for c in range(CH - 1):
                    dve.wait_ge(state_step, 4 * i + c)
                    dve.scalar_tensor_tensor(state[:, c + 1, :], state[:, c, :], bd, chunks(bank[2][:])[:, c, :],
                                             ALU.mult, ALU.add).then_inc(state_step, 1)
                dve.wait_ge(out_mm, i + 1)
                dve.wait_ge(acc_added, KD * i)
                for k in range(KD):
                    a = acc[:, k, bass.ds(b_prev * SB, SB)]
                    dve.tensor_tensor(a, a, bank[6 + k][:], ALU.add).then_inc(acc_added, 1)
                dve.wait_ge(o_mm, i + 1)
                dve.wait_ge(state_step, 4 * i + CH - 1)
                dve.scalar_tensor_tensor(state[:, 0, :], state[:, CH - 1, :], bd, chunks(bank[2][:])[:, CH - 1, :],
                                         ALU.mult, ALU.add).then_inc(state_step, 1)
                dve.wait_ge(tanh_done, i + 1)
                dve.wait_ge(o2_ready, i + 1)
                dve.scalar_tensor_tensor(og[:], tg[:], 1.0, bank[5][:], ALU.add, ALU.mult).then_inc(og_ready, 1)

            def step_end(i, b):
                dve.wait_ge(ssq_added, i)
                q = ssq[:, bass.ds(b * SB, SB)]
                dve.tensor_tensor(q, q, o2[:], ALU.add).then_inc(ssq_added, 1)
                dve.wait_ge(ogh_ready, i + 1)
                dve.tensor_tensor(ogl[:], og[:], ogh[:].bitcast(F32), ALU.subtract).then_inc(ogl_ready, 1)

            dve.wait_ge(zeroed, 6)
            dve.wait_ge(tab_ready, 3)
            split_low(0, 0)
            head_tables(0, 0)
            with dve.Fori(0, NH // 2) as hp:
                for par in range(2):
                    h = 2 * hp + par
                    step(h * NSB, NSB - 1, par, lambda i: 2 * h + 1)
                    step_end(h * NSB, 0)
                    split_low(h + 1, 1 - par)
                    head_tables((h + 1) % NH, 1 - par)
                    with dve.Fori(1, SB_PER_SEQ) as b:
                        step(h * NSB + b, b - 1, par, None)
                        step_end(h * NSB + b, b)
                    b = SB_PER_SEQ
                    step(h * NSB + b, b - 1, par, lambda i: 2 * h + 2)
                    step_end(h * NSB + b, b)
                    with dve.Fori(SB_PER_SEQ + 1, NSB) as b:
                        step(h * NSB + b, b - 1, par, None)
                        step_end(h * NSB + b, b)
            dve.wait_ge(out_mm, NSTEP + 1)
            for k in range(KD):
                a = acc[:, k, (NSB - 1) * SB:NSB * SB]
                dve.tensor_tensor(a, a, bank[6 + k][:], ALU.add).then_inc(acc_added, 1)

            dve.wait_ge(rms_mm, 1)
            dve.tensor_scalar(rmsv[:], bank[0][:, 0:NT], 1.0 / (NH * HD), RMS_EPS, ALU.mult, ALU.add).then_inc(rmsv_ready, 1)
            dve.wait_ge(swh_ready, 1)
            dve.tensor_tensor(swl[:], sraw[:], swh[:].bitcast(F32), ALU.subtract).then_inc(swl_ready, 1)

            def gated(t, u):
                dve.wait_ge(sg_ready, t + 1)
                dve.tensor_tensor(he[u][:], sg[u][:], bank[2 + u][:, F:2 * F], ALU.mult).then_inc(he_ready, 1)

            def gated_T(t, u):
                dve.wait_ge(hT_mm, t + 1)
                dve.tensor_copy(hT[u][:], bank[4 + u][0:F, 0:P]).then_inc(hT_ready, 1)

            def result(t, u, r, stored=None):
                dve.wait_ge(y_mm, t + 1)
                if stored is not None:
                    dve.wait_ge(y_stored[r], stored)
                dve.tensor_copy(ys[r][:], bank[6 + u][:, 0:D]).then_inc(ys_ready, 1)

            gated(0, 0)
            gated(1, 1)
            gated_T(0, 0)
            for t in range(RING):
                gated(t + 2, t % 2)
                gated_T(t + 1, (t + 1) % 2)
                result(t, t % 2, t)
            with dve.Fori(1, SLOT_TILES // RING - 1) as q:
                for r in range(RING):
                    t = q * RING + r
                    gated(t + 2, r % 2)
                    gated_T(t + 1, (r + 1) % 2)
                    result(t, r % 2, r, 16 * q)
            for r in range(RING):
                t = SLOT_TILES - RING + r
                if t + 2 < SLOT_TILES:
                    gated(t + 2, t % 2)
                if t + 1 < SLOT_TILES:
                    gated_T(t + 1, (t + 1) % 2)
                result(t, t % 2, r, 16 * (SLOT_TILES // RING - 1))

            for r in range(RING):
                dve.wait_ge(y_stored[r], 16 * SLOT_TILES // RING)
            dve.wait_ge(rms_ready, 1)
            with dve.Fori(0, NSB) as b:
                for ft in range(FT):
                    j = b * FT + ft
                    dve.wait_ge(ssg_ready, j + 1)
                    dve.tensor_tensor(sh[ft % 2][:], ssg[ft % 2][:], bank[2 + ft % 2][:], ALU.mult).then_inc(sh_ready, 1)
                    dve.wait_ge(shh_ready, j + 1)
                    dve.tensor_tensor(shl[:, ft, :], sh[ft % 2][:], shh[:, ft, :].bitcast(F32),
                                      ALU.subtract).then_inc(shl_ready, 1)
                for c in range(CH):
                    t = b * CH + c
                    r = c % 2
                    half = (c % 2) * D
                    dve.nop(nofuse=True)
                    dve.tensor_copy(cols[r][:, 0:1], at_col(rms, t)).then_inc(cols_ready, 1)
                    dve.tensor_copy(cols[r][:, 1:1 + TOPK], at_col(wgt, t)).then_inc(cols_ready, 1)
                    dve.wait_ge(cols_ready, 2 * (t + 1))
                    dve.wait_ge(xr_loaded[r], 16 * (b * 2 + c // 2 + 1))
                    dve.wait_ge(out_stored[r], 16 * (b * 2 + c // 2))
                    if c == 0:
                        dve.wait_ge(accT_mm, b + 1)
                    n = 6 * t
                    dve.scalar_tensor_tensor(res[r][:], bank[6 + c // 2][:, half:half + D], cols[r][:, 0:1], xr[r][:],
                                             ALU.mult, ALU.add).then_inc(summed, 1)
                    dve.wait_ge(summed, n + 1)
                    if c == 0:
                        dve.wait_ge(down_mm, b + 1)
                    dve.tensor_tensor(res[r][:], res[r][:], bank[4 + c // 2][:, half:half + D], ALU.add).then_inc(summed, 1)
                    dve.wait_ge(gathered[r], 16 * TOPK * (b * 2 + c // 2 + 1))
                    for k in range(TOPK):
                        dve.wait_ge(summed, n + 2 + k)
                        dve.scalar_tensor_tensor(res[r][:], yk[r][:, k, :], cols[r][:, 1 + k:2 + k], res[r][:],
                                                 ALU.mult, ALU.add).then_inc(summed, 1)

        @block.tensor
        def _(pe):
            def split_product(out_, lhs, rhs, last=True):
                (lh, ll), (rh, rl) = lhs, rhs
                pe.matmul(out_, lh, rh, start=True, stop=False)
                pe.matmul(out_, lh, rl, start=False, stop=False)
                return pe.matmul(out_, ll, rh, start=False, stop=last)

            pe.wait_ge(pool_step, 9)
            pe.wait_ge(dve_const, 2)
            pe.wait_ge(consts_loaded, 48)
            with pe.Fori(0, NSB // 2) as g2:
                for u in range(2):
                    g = g2 * 2 + u
                    pe.wait_ge(xn_ready, CH * (g + 1))
                    pe.wait_ge(xl_ready, KD * g)
                    for k in range(KD):
                        for c in range(CH):
                            mm = pe.transpose(bank[k][:, c * P:(c + 1) * P], xn[u][:, c, k * P:(k + 1) * P], ident[:])
                    mm.then_inc(xT_mm, 1)
                    pe.wait_ge(xf_ready, KD * (g + 1))
                    pe.wait_ge(lc_ready, g)
                    for c in range(CH):
                        for k in range(KD):
                            mm = pe.matmul(bank[2][:, c * E:(c + 1) * E], xf[:, k, c * P:(c + 1) * P], rw[:, k, :],
                                           start=(k == 0), stop=(k == KD - 1))
                    mm.then_inc(logits_mm, 1)
                    pe.wait_ge(mask_ready, g + 1)
                    pe.wait_ge(macc_ready, g + 1)
                    for c in range(CH):
                        o = bank[3][:, c * E:(c + 1) * E]
                        pe.matmul(o, upper[:], mask[:, c, :], start=True, stop=False)
                        for j in range(c):
                            pe.matmul(o, ones_bf[:], mask[:, j, :], start=False, stop=False)
                        mm = pe.matmul(o, ones_bf[:], macc[:], start=False, stop=True)
                    mm.then_inc(rank_mm, 1)
            pe.wait_ge(macc_ready, NSB + 1)
            pe.matmul(bank[4][:, 0:E], ones_bf[:], macc[:], start=True, stop=True).then_inc(tot_mm, 1)
            pe.wait_ge(ecl_ready, 1)
            for j in range(2):
                mm = pe.matmul(bank[5][0:1, j * P:(j + 1) * P], ecl[:, j:j + 1], ident[:], start=True, stop=True)
            mm.then_inc(etab_mm, 1)

            def project(dst, par, which, b):
                for k in range(KD):
                    cols_ = slice((k * 4 + which) * P, (k * 4 + which + 1) * P)
                    tok = bass.ds(b * SB, SB)
                    lh, ll = wh[par][:, cols_], wl[par][:, cols_]
                    rh, rl = xh[:, k, tok], xl[:, k, tok]
                    pe.matmul(dst, lh, rh, start=(k == 0), stop=False)
                    pe.matmul(dst, lh, rl, start=False, stop=False)
                    mm = pe.matmul(dst, ll, rh, start=False, stop=(k == KD - 1))
                return mm

            def project_out(par):
                for f in range(KD):
                    cols_ = slice(WC + f * P, WC + (f + 1) * P)
                    lh, ll = wh[par][:, cols_], wl[par][:, cols_]
                    mm = split_product(bank[6 + f][:], (lh, ll), (ogh[:], ogl[:]))
                return mm

            def step(i, b, par, par_prev):
                ch = [slice(c * P, (c + 1) * P) for c in range(CH)]
                pe.wait_ge(tanh_done, i)
                project(bank[0][:], par, 1, b).then_inc(k_mm, 1)
                pe.wait_ge(sm_ready, i)
                project(bank[1][:], par, 2, b).then_inc(v_mm, 1)
                pe.wait_ge(state_step, 4 * i)
                project(bank[2][:], par, 0, b).then_inc(q_mm, 1)
                pe.wait_ge(k_silu, i + 1)
                for c in range(CH):
                    mm = pe.transpose(bank[3][:, ch[c]], kT[:, ch[c]], ident[:])
                mm.then_inc(kT_mm, 1)
                pe.wait_ge(v_silu, i + 1)
                for c in range(CH):
                    mm = pe.transpose(bank[4][:, ch[c]], vT[:, ch[c]], ident[:])
                mm.then_inc(vT_mm, 1)
                project(bank[0][:], par, 3, b).then_inc(g_mm, 1)
                pe.wait_ge(q_silu, i + 1)
                for c in range(CH):
                    mm = pe.matmul(bank[1][:, ch[c]], kT[:, ch[c]], qT[:, ch[c]], start=True, stop=True)
                mm.then_inc(s_mm, 1)
                pe.wait_ge(kp_ready, i + 1)
                pe.wait_ge(vt_ready, i + 1)
                for c in range(CH):
                    mm = pe.matmul(bank[2][:, ch[c]], kp[:, ch[c]], vt[:, ch[c]], start=True, stop=True)
                mm.then_inc(kv_mm, 1)
                if i is not None:
                    pe.wait_ge(ogl_ready, i)
                pe.wait_ge(acc_added, KD * i)
                project_out(par_prev).then_inc(out_mm, 1)
                pe.wait_ge(sm_ready, i + 1)
                pe.wait_ge(qp_ready, i + 1)
                pe.wait_ge(state_step, 4 * i + CH - 1)
                pe.wait_ge(og_ready, i)
                pe.wait_ge(o2_ready, i)
                for c in range(CH):
                    pe.matmul(bank[5][:, ch[c]], vt[:, ch[c]], sm[:, ch[c]], start=True, stop=False)
                    mm = pe.matmul(bank[5][:, ch[c]], state[:, c, :], qp[:, ch[c]], start=False, stop=True)
                mm.then_inc(o_mm, 1)

            pe.wait_ge(zeroed, 6)
            with pe.Fori(0, NH // 2) as hp:
                for par in range(2):
                    h = 2 * hp + par
                    pe.wait_ge(w_ready, h + 1)
                    step(h * NSB, 0, par, 1 - par)
                    with pe.Fori(1, NSB) as b:
                        step(h * NSB + b, b, par, par)
            pe.wait_ge(ogl_ready, NSTEP)
            pe.wait_ge(acc_added, KD * NSTEP)
            project_out(1).then_inc(out_mm, 1)

            pe.wait_ge(ssq_added, NSTEP)
            for t in range(NT):
                mm = pe.matmul(bank[0][:, t:t + 1], ssq[:, t * P:(t + 1) * P], ones[:], start=True, stop=True)
            mm.then_inc(rms_mm, 1)
            pe.wait_ge(rmsv_ready, 1)
            pe.wait_ge(acc_added, KD * (NSTEP + 1))

            def turn(t, u, r, loaded):
                pe.wait_ge(tile_loaded[r], loaded)
                for k in range(KD):
                    mm = pe.transpose(bank[u][:, k * P:(k + 1) * P], xs[r][:, k * P:(k + 1) * P], ident[:])
                mm.then_inc(xsT_mm, 1)

            def gate_up(t, u, r):
                pe.wait_ge(xsT_ready, t + 1)
                for k in range(KD):
                    mm = pe.matmul(bank[2 + u][:, 0:2 * F], xsT[u][:, k, :], gu[r][:, k, :],
                                   start=(k == 0), stop=(k == KD - 1))
                mm.then_inc(gu_mm, 1)

            def turn_gated(t, u):
                pe.wait_ge(he_ready, t + 1)
                pe.nop(nofuse=True)
                pe.transpose(bank[4 + u][0:F, 0:P], he[u][:], ident[:]).then_inc(hT_mm, 1)

            def down(t, u, r):
                pe.wait_ge(hT_ready, t + 1)
                if not isinstance(t, int) or t >= 2:
                    pe.wait_ge(ys_ready, t - 1)
                pe.matmul(bank[6 + u][:, 0:D], hT[u][:], wde[r][:], start=True, stop=True).then_inc(y_mm, 1)

            for t in range(3):
                turn(t, t % 2, t, 48)
                if t >= 1:
                    gate_up(t - 1, (t - 1) % 2, t - 1)
                if t >= 2:
                    turn_gated(t - 2, t % 2)
            turn(3, 1, 3, 48)
            gate_up(2, 0, 2)
            turn_gated(1, 1)
            down(0, 0, 0)
            with pe.Fori(1, SLOT_TILES // RING) as q:
                for r in range(RING):
                    t = q * RING + r
                    turn(t, r % 2, r, 48 * (q + 1))
                    gate_up(t - 1, (r - 1) % 2, (r - 1) % RING)
                    turn_gated(t - 2, r % 2)
                    down(t - 3, (r - 3) % 2, (r - 3) % RING)
            t = SLOT_TILES
            gate_up(t - 1, 1, 3)
            turn_gated(t - 2, 0)
            down(t - 3, 1, 1)
            turn_gated(t - 1, 1)
            down(t - 2, 0, 2)
            down(t - 1, 1, 3)

            pe.wait_ge(swl_ready, 1)
            pe.wait_ge(ys_ready, SLOT_TILES)
            with pe.Fori(0, NSB) as b:
                tok = bass.ds(b * SB, SB)
                for ft in range(FT):
                    j = b * FT + ft
                    if ft >= 2:
                        pe.wait_ge(sh_ready, j - 1)
                    else:
                        pe.wait_ge(sh_ready, b * FT)
                    for i in range(2):
                        dst = bank[2 * i + ft % 2][:]
                        for k in range(KD):
                            c0 = (i * KD + k) * 512 + ft * P
                            lh, ll = swh[:, c0:c0 + P], swl[:, c0:c0 + P]
                            pe.matmul(dst, lh, xh[:, k, tok], start=(k == 0), stop=False)
                            pe.matmul(dst, lh, xl[:, k, tok], start=False, stop=False)
                            mm = pe.matmul(dst, ll, xh[:, k, tok], start=False, stop=(k == KD - 1))
                    mm.then_inc(sgu_mm, 1)
                pe.wait_ge(accs_ready, KD * (b + 1))
                pe.wait_ge(summed, 6 * CH * b)
                for c in range(CH):
                    for k in range(KD):
                        mm = pe.transpose(bank[6 + c // 2][:, (c % 2) * D + k * P:(c % 2) * D + (k + 1) * P],
                                          accs[:, k, c * P:(c + 1) * P], ident[:])
                mm.then_inc(accT_mm, 1)
                pe.wait_ge(shl_ready, FT * (b + 1))
                for c in range(CH):
                    dst = bank[4 + c // 2][:, (c % 2) * D:(c % 2 + 1) * D]
                    for ft in range(FT):
                        c0 = 2 * KD * 512 + ft * D
                        rh, rl = swh[:, c0:c0 + D], swl[:, c0:c0 + D]
                        lh, ll = shh[:, ft, c * P:(c + 1) * P], shl[:, ft, c * P:(c + 1) * P]
                        pe.matmul(dst, lh, rh, start=(ft == 0), stop=False)
                        pe.matmul(dst, lh, rl, start=False, stop=False)
                        mm = pe.matmul(dst, ll, rh, start=False, stop=(ft == FT - 1))
                mm.then_inc(down_mm, 1)


def kernel(**inputs):
    import numpy as np
    import concourse.bacc as bacc
    from concourse.bass_utils import run_bass_kernel_spmd as run

    a = {k: np.asarray(v) for k, v in inputs.items()}
    feats = a["L0_attn_w_qkv"].reshape(NH, 3, HD, KD, P)
    gates = a["L0_attn_w_gate"].reshape(NH, HD, KD, P)
    wg = a["L0_ffn_wg"].reshape(E, KD, P, F)
    wu = a["L0_ffn_wu"].reshape(E, KD, P, F)
    arrays = {
        "x_rows": a["L0_attn_hidden_states"].reshape(T, D),
        "slope_row": a["L0_attn_slope_rate"].reshape(NH),
        "wqkv_in": feats.transpose(0, 4, 3, 1, 2).reshape(NH, P, KD, 3 * HD),
        "wgate_in": gates.transpose(0, 3, 2, 1),
        "wout_in": a["L0_attn_w_out"].reshape(D, NH, HD).transpose(1, 2, 0),
        "norm_in": a["L0_attn_norm_w"].reshape(NH, HD, 1),
        "router_in": a["L0_ffn_router_w"],
        "bias_in": a["L0_ffn_router_bias"],
        "wgu_in": np.stack([wg, wu], axis=3).transpose(0, 2, 1, 3, 4).reshape(E, P, KD, 2 * F),
        "wd_in": a["L0_ffn_wd"],
        "swg_in": a["L0_ffn_swg"],
        "swu_in": a["L0_ffn_swu"],
        "swd_in": a["L0_ffn_swd"],
    }
    arrays = {k: np.ascontiguousarray(v) for k, v in arrays.items()}
    nc = bacc.Bacc("TRN2", target_bir_lowering=False, num_devices=1)
    args = [nc.dram_tensor(k, v.shape, mybir.dt.from_np(v.dtype), kind="ExternalInput").ap() for k, v in arrays.items()]
    args.append(nc.dram_tensor("out_rows", (T, D), F32, kind="ExternalOutput").ap())
    lightning_moe(nc, *args)
    r = run(nc, [arrays], core_ids=[0])
    return r.results[0]["out_rows"].reshape(B, N, D)
```

```python
from contextlib import ExitStack

import concourse.bass as bass
from concourse import mybir

F32 = mybir.dt.float32
F32R = mybir.dt.float32r
BF16 = mybir.dt.bfloat16
I32 = mybir.dt.int32
U32 = mybir.dt.uint32
ALU = mybir.AluOpType
ACT = mybir.ActivationFunctionType
AX = mybir.AxisListType

P = 128
B, N, D = 2, 2048, 256
T = B * N
KD = D // P
NH, HD = 16, 128
SB = 512
NSB = T // SB
CH = SB // P
SB_PER_SEQ = N // SB
NT = T // P
E, F, TOPK = 64, 64, 4
SLOT_TILES = T * TOPK // P + E
S, HS = 2, 256
FT = S * HS // P
LN_EPS = 1e-5
RMS_EPS = 1e-6
NSTEP = NH * NSB
SW = 2 * KD * 512 + FT * D
PLAIN, GATHER = 2, 8
NPAIR = SLOT_TILES // 2
assert NPAIR == 2 * (GATHER - PLAIN) * NSB and NT == CH * (NH - GATHER)
WE = KD * 2 * F + P
GU = ((4, 5), (0, 1))
LINKS = 17
WC = KD * 4 * P
TAB = 2 * P + 2


def lightning_moe(nc, x, slope, wqkv, wgate, wout, norm_w, router_w, router_bias,
                  wexp, swg, swu, swd, out):
    xn_dram = nc.dram_tensor("xn_rows", [T, D], F32, kind="Internal").ap()
    slot_x = nc.dram_tensor("slot_x", [SLOT_TILES * P, D], F32, kind="Internal").ap()
    slot_y = nc.dram_tensor("slot_y", [SLOT_TILES * P, D], F32, kind="Internal").ap()
    part = nc.dram_tensor("part", [T, D], F32, kind="Internal").ap()
    part2 = nc.dram_tensor("part2", [T, D], F32, kind="Internal").ap()

    top = ExitStack()
    with top:
        def sem(name):
            return top.enter_context(nc.semaphore(name))

        def sb_in(stack):
            return lambda name, shape, dt=F32: stack.enter_context(nc.sbuf_tensor(name, shape, dt))

        bank = [top.enter_context(nc.psum_tensor(f"bank{i}", [P, 512], F32)) for i in range(8)]
        keep = sb_in(top)
        xh = keep("xh", [P, KD, T], F32R)
        xl = keep("xl", [P, KD, T], F32R)
        ident = keep("ident", [P, P])
        ones = keep("ones", [P, 1])
        pos = keep("pos", [P, NT, TOPK], U32)
        wgt = keep("wgt", [P, NT, TOPK])
        etab = keep("etab", [1, 2 * P], I32)
        tab = keep("tab", [P, NH, TAB])
        raw = keep("raw", [P, WC + D + 1])
        rms = keep("rms", [P, NT])
        rmsv = keep("rmsv", [P, NT])
        mhalf2 = keep("mhalf2", [P, NT])
        zeros = keep("zeros", [P, 2 * D])

        with ExitStack() as st:
            sb = sb_in(st)
            xin = [sb(f"xin{i}", [P, CH, D]) for i in range(2)]
            xn = [sb(f"xn{i}", [P, CH, D]) for i in range(2)]
            xf = sb("xf", [P, KD, SB])
            rw = sb("rw", [P, KD, E])
            rbias = sb("rbias", [P, E])
            stat = sb("stat", [P, CH, 6])
            mv = sb("mv", [P, CH, 2])
            ve = sb("ve", [P, CH])
            rs = sb("rs", [P, CH])
            mhalf = sb("mhalf", [P, CH])
            upper = sb("upper", [P, P], BF16)
            ones_bf = sb("ones_bf", [P, P], BF16)
            iota_e = sb("iota_e", [P, E])
            lgb = sb("lgb", [P, CH, E])
            m8 = sb("m8", [P, CH, 8])
            i8 = sb("i8", [P, CH, 8], U32)
            idxf = sb("idxf", [P, CH * TOPK])
            mx = sb("mx", [P, CH])
            lc = sb("lc", [P, CH, E])
            pr = sb("pr", [P, CH, E])
            z = sb("z", [P, CH])
            zi = sb("zi", [P, CH])
            oh = sb("oh", [P, NT * TOPK, E], BF16)
            prod = sb("prod", [P, CH * TOPK, E])
            pk = sb("pk", [P, CH, TOPK])
            pz = sb("pz", [P, CH, TOPK])
            ps4 = sb("ps4", [P, CH])
            pi4 = sb("pi4", [P, CH])
            mask = sb("mask", [P, CH, E], BF16)
            mgrp = sb("mgrp", [P, E])
            macc = sb("macc", [P, E], BF16)
            rank = sb("rank", [P, NT * TOPK])
            posf = sb("posf", [P, NT * TOPK])
            tot_a = sb("tot_a", [P, E], I32)
            tot_s = sb("tot_s", [P, E], I32)
            cnt = sb("cnt", [P, E])
            incl = sb("incl", [P, E])
            base = sb("base", [P, E])
            base2 = sb("base2", [P, E])
            zero_e = sb("zero_e", [P, E])
            tcol = sb("tcol", [P, 2])
            le = sb("le", [P, 2, E])
            ecol = sb("ecol", [P, 2])
            ecl = sb("ecl", [P, 2])
            slope_b = sb("slope_b", [P, NH])
            ns_all = sb("ns_all", [P, NH])
            dm = sb("dm", [P, P])
            dm0 = sb("dm0", [P, P])
            mrow = sb("mrow", [P, P])
            kcol = sb("kcol", [P, NH])
            karg = sb("karg", [P, NH])
            swh = sb("swh", [P, SW], F32R)
            swl = sb("swl", [P, SW], F32R)
            sraw = sb("sraw", [P, SW])
            ssg = sb("ssg", [P, SB])
            sh = sb("sh", [P, SB])
            shh = sb("shh", [P, FT, SB], F32R)
            shl = sb("shl", [P, FT, SB], F32R)
            res4 = sb("res4", [P, CH, D])

        acc = keep("acc", [P, KD, T])
        ssq = keep("ssq", [P, T])
        wh = [keep(f"wh{i}", [P, WC + D], F32R) for i in range(2)]
        wl = [keep(f"wl{i}", [P, WC + D], F32R) for i in range(2)]
        wos = keep("wos", [P, D])
        hc = [keep(f"hc{i}", [P, TAB]) for i in range(2)]
        kT = keep("kT", [P, SB])
        vT = keep("vT", [P, SB])
        qT = keep("qT", [P, SB])
        tg = keep("tg", [P, SB])
        kp = keep("kp", [P, SB])
        vt = keep("vt", [P, SB])
        sm = keep("sm", [P, SB])
        qp = keep("qp", [P, SB])
        o2 = keep("o2", [P, SB])
        og = keep("og", [P, SB])
        ogh = keep("ogh", [P, SB], F32R)
        ogl = keep("ogl", [P, SB], F32R)
        state = keep("state", [P, CH, HD])
        with ExitStack() as st:
            sb = sb_in(st)
            row = sb("row", [P, CH, D])
            cur_pos = [sb(f"cur_pos{r}", [P, TOPK], U32) for r in range(CH)]
        with ExitStack() as st:
            sb = sb_in(st)
            xs = [sb(f"xs{i}", [P, 2, D]) for i in range(2)]
            we = [sb(f"we{i}", [P, 2, WE]) for i in range(2)]
            xsT = sb("xsT", [P, 2, KD, P])
            sg = sb("sg", [P, 2, F])
            he = sb("he", [P, 2, 2, F])
            hT = sb("hT", [P, 2, P])
            ys = [sb(f"ys{i}", [P, 2, D]) for i in range(2)]
        with ExitStack() as st:
            sb = sb_in(st)
            yk = [sb(f"yk{i}", [P, TOPK, D]) for i in range(2)]
            xr = [sb(f"xr{i}", [P, D]) for i in range(2)]
            cols = sb("cols", [P, TOPK])
            picked = [sb(f"picked{i}", [P, TOPK], U32) for i in range(2)]
        accs, res = (kT, vT), (qT, tg, kp, vt)

        consts_loaded = sem("consts_loaded")
        sraw_loaded = sem("sraw_loaded")
        pool_step = sem("pool_step")
        dve_const = sem("dve_const")
        tables = sem("tables")
        tab_ready = sem("tab_ready")
        x_loaded = [sem(f"x_loaded{u}") for u in range(2)]
        slots_zero = sem("slots_zero")
        stats_done = sem("stats_done")
        aggr_done = sem("aggr_done")
        var_ready = sem("var_ready")
        rstd_ready = sem("rstd_ready")
        xn_ready = sem("xn_ready")
        xn_stored = [sem(f"xn_stored{u}") for u in range(2)]
        xT_mm = sem("xT_mm")
        xf_ready = sem("xf_ready")
        xh_ready = sem("xh_ready")
        xl_ready = sem("xl_ready")
        logits_mm = sem("logits_mm")
        route = sem("route")
        lc_ready = sem("lc_ready")
        pr_ready = sem("pr_ready")
        oh_ready = sem("oh_ready")
        prod_ready = sem("prod_ready")
        mask_ready = sem("mask_ready")
        rank_mm = sem("rank_mm")
        macc_ready = sem("macc_ready")
        tot_mm = sem("tot_mm")
        etab_mm = sem("etab_mm")
        ecl_ready = sem("ecl_ready")
        routed = sem("routed")
        swh_ready = sem("swh_ready")
        swl_ready = sem("swl_ready")
        sgu_mm = sem("sgu_mm")
        ssg_ready = sem("ssg_ready")
        sh_ready = sem("sh_ready")
        shh_ready = sem("shh_ready")
        shl_ready = sem("shl_ready")
        down_mm = sem("down_mm")
        part_ready = sem("part_ready")
        part_stored = sem("part_stored")
        raw_loaded = sem("raw_loaded")
        wos_ready = sem("wos_ready")
        wh_ready = sem("wh_ready")
        w_ready = sem("w_ready")
        zeroed = sem("zeroed")
        k_mm = sem("k_mm")
        v_mm = sem("v_mm")
        q_mm = sem("q_mm")
        kT_mm = sem("kT_mm")
        vT_mm = sem("vT_mm")
        g_mm = sem("g_mm")
        s_mm = sem("s_mm")
        kv_mm = sem("kv_mm")
        out_mm = sem("out_mm")
        o_mm = sem("o_mm")
        k_silu = sem("k_silu")
        v_silu = sem("v_silu")
        q_silu = sem("q_silu")
        vt_ready = sem("vt_ready")
        tanh_done = sem("tanh_done")
        o2_ready = sem("o2_ready")
        ogh_ready = sem("ogh_ready")
        ogl_ready = sem("ogl_ready")
        qp_ready = sem("qp_ready")
        kp_ready = sem("kp_ready")
        sm_ready = sem("sm_ready")
        state_step = sem("state_step")
        state_zero = sem("state_zero")
        acc_added = sem("acc_added")
        og_ready = sem("og_ready")
        ssq_added = sem("ssq_added")
        row_loaded = [sem(f"row_loaded{r}") for r in range(CH)]
        idx_copied = sem("idx_copied")
        scattered = [sem(f"scattered{r}") for r in range(CH)]
        pair_loaded = [sem(f"pair_loaded{r}") for r in range(2)]
        xsT_mm = sem("xsT_mm")
        xsT_ready = sem("xsT_ready")
        gu_mm = sem("gu_mm")
        sg_ready = sem("sg_ready")
        he_ready = sem("he_ready")
        hT_mm = sem("hT_mm")
        hT_ready = sem("hT_ready")
        y_mm = sem("y_mm")
        ys_ready = sem("ys_ready")
        y_stored = [sem(f"y_stored{r}") for r in range(2)]
        cols_ready = sem("cols_ready")
        xr_loaded = [sem(f"xr_loaded{r}") for r in range(2)]
        picked_ready = sem("picked_ready")
        gathered = [sem(f"gathered{r}") for r in range(2)]
        summed = sem("summed")
        part2_stored = [sem(f"part2_stored{r}") for r in range(2)]
        rms_mm = sem("rms_mm")
        rmsv_ready = sem("rmsv_ready")
        rms_ready = sem("rms_ready")
        accs_ready = sem("accs_ready")
        accT_mm = sem("accT_mm")
        final = sem("final")
        res_loaded = [sem(f"res_loaded{r}") for r in range(4)]
        out_stored = [sem(f"out_stored{r}") for r in range(4)]

        x_grp = x.rearrange("(g c p) d -> g p c d", c=CH, p=P)
        xn_grp = xn_dram.rearrange("(g c p) d -> g p c d", c=CH, p=P)
        part_grp = part.rearrange("(g c p) d -> g p c d", c=CH, p=P)
        xn_tile = xn_dram.rearrange("(t p) d -> t p d", p=P)
        part_tile = part.rearrange("(t p) d -> t p d", p=P)
        part2_tile = part2.rearrange("(t p) d -> t p d", p=P)
        part2_pair = part2.rearrange("(t c p) d -> t p c d", c=2, p=P)
        out_pair = out.rearrange("(t c p) d -> t p c d", c=2, p=P)
        slot_x_pair = slot_x.rearrange("(t c p) d -> t p c d", c=2, p=P)
        slot_y_pair = slot_y.rearrange("(t c p) d -> t p c d", c=2, p=P)
        zero_parts = slot_x.rearrange("(q p n r) d -> q p n (r d)", q=4, p=P, r=2)

        def at(ap, i):
            rest = " ".join("abc"[1:len(ap.shape) - 1])
            return ap[bass.ds(i, 1)].rearrange(f"o a {rest} -> (o a) {rest}")

        def at_col(tensor, i):
            return tensor[:, bass.ds(i, 1), :].rearrange("p o n -> p (o n)")

        def chunks(ap):
            return ap.rearrange("p (c m) -> p c m", c=CH)

        def per_chunk(ap):
            return ap.unsqueeze(1).to_broadcast([P, CH, ap.shape[-1]])

        def halves(tensor):
            return tensor[:].rearrange("p (c d) -> p c d", c=2)

        def heads(eng, first_pair, last_pair, head):
            with eng.Fori(first_pair, last_pair) as hp:
                for par in range(2):
                    head(2 * hp + par, par)

        block = top.enter_context(nc.Block())

        @block.sync
        def _(sp):
            sp.dma_start(xin[0][:], x_grp[0]).then_inc(x_loaded[0], 16)
            for dst, src in ((rw[:], router_w.rearrange("(k p) e -> p k e", p=P)),
                             (rbias[:], router_bias.partition_broadcast(P)),
                             (slope_b[:], slope.partition_broadcast(P))):
                sp.dma_start(dst, src).then_inc(consts_loaded, 16)
            w = sraw[:, 0:2 * KD * 512].rearrange("p (i k s h) -> p i k s h", i=2, k=KD, s=S)
            for i, src in enumerate((swg, swu)):
                for s in range(S):
                    sp.dma_start(w[:, i, :, s, :], src[s].rearrange("(k p) h -> p k h", p=P)).then_inc(sraw_loaded, 16)
            sp.dma_start(sraw[:, 2 * KD * 512:].rearrange("p (t d) -> p t d", d=D),
                         swd.rearrange("s (t p) d -> p (s t) d", p=P)).then_inc(sraw_loaded, 16)
            sp.dma_start(xin[1][:], x_grp[1]).then_inc(x_loaded[1], 16)

            def group(g, g2, u, more):
                sp.wait_ge(xn_ready, CH * (g + 1))
                sp.dma_start(at(xn_grp, g), xn[u][:]).then_inc(xn_stored[u], 16)
                sp.wait_ge(part_ready, CH * (g + 1))
                sp.dma_start(at(part_grp, g), res4[:]).then_inc(part_stored, 16)
                if more:
                    sp.dma_start(xin[u][:], at(x_grp, g + 2)).then_inc(x_loaded[u], 16)

            sp.wait_ge(dve_const, 1)
            for q in range(4):
                sp.dma_start(zero_parts[q], zeros[:].unsqueeze(1).to_broadcast([P, SLOT_TILES // 8, 2 * D])).then_inc(slots_zero, 16)
            with sp.Fori(0, NSB // 2 - 1) as g2:
                for u in range(2):
                    group(g2 * 2 + u, g2, u, True)
            for u in range(2):
                group(NSB - 2 + u, NSB // 2 - 1, u, False)

            def load_head(h):
                w = raw[:, 0:WC].rearrange("p (k n) -> p k n", k=KD)
                sp.dma_start(w[:, :, 0:3 * HD], at(wqkv, h)).then_inc(raw_loaded, 16)
                sp.dma_start(w[:, :, 3 * HD:4 * HD], at(wgate, h)).then_inc(raw_loaded, 16)
                sp.dma_start(raw[:, WC:WC + D], at(wout, h)).then_inc(raw_loaded, 16)
                sp.dma_start(raw[:, WC + D:WC + D + 1], at(norm_w, h)).then_inc(raw_loaded, 16)

            def next_head(h):
                sp.wait_ge(w_ready, h + 1)
                load_head((h + 1) % NH)

            load_head(0)
            heads(sp, 0, PLAIN // 2, lambda h, par: next_head(h))

            for r in range(CH):
                sp.wait_ge(scattered[r], 16 * TOPK * NT // CH)

            def load_pair(q, r):
                sp.dma_start(xs[r][:], at(slot_x_pair, q)).then_inc(pair_loaded[r], 16)
                for j in range(2):
                    e = sp.value_load(etab[0:1, bass.ds(q * 2 + j, 1)], min_val=0, max_val=E - 1)
                    sp.dma_start(we[r][:, j, :], at(wexp, e)).then_inc(pair_loaded[r], 16)

            def expert_step(m, more):
                for r in range(2):
                    q = 2 * m + r
                    sp.wait_ge(y_mm, q + 1)
                    if more:
                        load_pair(q + 2, r)
                    sp.wait_ge(ys_ready, q + 1)
                    sp.dma_start(at(slot_y_pair, q), ys[r][:]).then_inc(y_stored[r], 16)

            for r in range(2):
                load_pair(r, r)

            def expert_head(h, par):
                next_head(h)
                expert_step((h - PLAIN) * NSB, True)
                with sp.Fori(1, NSB) as b:
                    expert_step((h - PLAIN) * NSB + b, True)

            heads(sp, PLAIN // 2, GATHER // 2 - 1, expert_head)
            expert_head(GATHER - 2, 0)
            m = (GATHER - 1 - PLAIN) * NSB
            next_head(GATHER - 1)
            expert_step(m, True)
            with sp.Fori(1, NSB - 1) as b:
                expert_step(m + b, True)
            expert_step(m + NSB - 1, False)
            for r in range(2):
                sp.wait_ge(y_stored[r], 16 * NPAIR // 2)

            def gather_head(h, par):
                next_head(h)
                t0 = (h - GATHER) * CH
                for c2 in range(2):
                    for r in range(2):
                        sp.wait_ge(part2_stored[r], 16 * ((h - GATHER) * 2 + c2))
                        sp.dma_start(xr[r][:], at(part_tile, t0 + 2 * c2 + r)).then_inc(xr_loaded[r], 16)
                    for r in range(2):
                        sp.wait_ge(summed, TOPK * (t0 + 2 * c2 + r + 1))
                        sp.dma_start(at(part2_tile, t0 + 2 * c2 + r), xr[r][:]).then_inc(part2_stored[r], 16)

            for u in range(1):
                sp.wait_ge(part_stored, 16 * NSB)
            heads(sp, GATHER // 2, NH // 2, gather_head)

            sp.wait_ge(out_mm, KD * (NSTEP + 1))
            sp.wait_ge(og_ready, NSTEP)
            for r in range(2):
                sp.wait_ge(part2_stored[r], 16 * NT // 2)

            for r in range(4):
                sp.dma_start(halves(res[r]), part2_pair[r]).then_inc(res_loaded[r], 16)
            with sp.Fori(0, NT // 8 - 1) as q:
                for r in range(4):
                    sp.wait_ge(final, 8 * q + 2 * (r + 1))
                    sp.dma_start(at(out_pair, q * 4 + r), halves(res[r])).then_inc(out_stored[r], 16)
                for r in range(4):
                    sp.wait_ge(out_stored[r], 16 * (q + 1))
                    sp.dma_start(halves(res[r]), at(part2_pair, q * 4 + 4 + r)).then_inc(res_loaded[r], 16)
            for r in range(4):
                sp.wait_ge(final, NT - 8 + 2 * (r + 1))
                sp.dma_start(out_pair[NT // 2 - 4 + r], halves(res[r])).then_inc(out_stored[r], 16)
            for r in range(4):
                sp.wait_ge(out_stored[r], 16 * NT // 8)

        @block.gpsimd
        def _(pool):
            exact = dict(allow_small_or_imprecise_dtypes=True)
            pool.memset(ident[:], 0.0).then_inc(pool_step, 1)
            pool.memset(upper[:], 1.0).then_inc(pool_step, 1)
            pool.iota(dm[:], [[1, P]], base=0, channel_multiplier=-1, **exact).then_inc(pool_step, 1)
            pool.iota(mrow[:], [[1, P]], base=1, channel_multiplier=0, **exact).then_inc(pool_step, 1)
            pool.iota(kcol[:], [[0, NH]], base=P - 1, channel_multiplier=-1, **exact).then_inc(pool_step, 1)
            pool.iota(iota_e[:], [[1, E]], base=0, channel_multiplier=0, **exact).then_inc(pool_step, 1)
            pool.iota(tcol[:], [[P, 2]], base=0, channel_multiplier=1, **exact).then_inc(pool_step, 1)
            pool.wait_ge(pool_step, 7)
            pool.affine_select(out=ident[:], in_=ident[:], pattern=[[-1, P]], compare_op=ALU.not_equal, fill=1.0,
                               base=0, channel_multiplier=1).then_inc(pool_step, 1)
            pool.affine_select(out=upper[:], in_=upper[:], pattern=[[1, P]], compare_op=ALU.is_gt, fill=0.0,
                               base=0, channel_multiplier=-1).then_inc(pool_step, 1)
            pool.wait_ge(dve_const, 2)

            def normalise(g, g2, u):
                pool.wait_ge(var_ready, g + 1)
                pool.tensor_tensor(rs[:], ve[:], mhalf[:], ALU.pow).then_inc(rstd_ready, 1)
                pool.wait_ge(rstd_ready, g + 1)
                pool.wait_ge(xn_stored[u], 16 * g2)
                pool.wait_ge(xT_mm, g)
                pool.nop(nofuse=True)
                for c in range(CH):
                    pool.tensor_scalar(xn[u][:, c, :], xin[u][:, c, :], mv[:, c, 0:1], rs[:, c:c + 1],
                                       ALU.subtract, ALU.mult).then_inc(xn_ready, 1)

            normalise(0, 0, 0)
            pool.wait_ge(tables, 2 * NH)
            pool.affine_select(out=tab[:, :, 0:P], in_=tab[:, :, 0:P], pattern=[[0, NH], [1, P]], compare_op=ALU.is_ge,
                               fill=0.0, base=0, channel_multiplier=-1).then_inc(tab_ready, 1)
            normalise(1, 0, 1)
            with pool.Fori(1, NSB // 2) as g2:
                for u in range(2):
                    normalise(g2 * 2 + u, g2, u)

            pool.wait_ge(routed, 2)
            pool.wait_ge(part_stored, 16 * NSB)
            for u in range(2):
                pool.wait_ge(xn_stored[u], 16 * NSB // 2)
            pool.memset(wh[1][:, WC:WC + D].bitcast(F32), 0.0).then_inc(zeroed, 1)
            pool.memset(wl[1][:, WC:WC + D].bitcast(F32), 0.0).then_inc(zeroed, 1)
            pool.memset(ogh[:].bitcast(F32), 0.0).then_inc(zeroed, 1)
            pool.memset(ogl[:].bitcast(F32), 0.0).then_inc(zeroed, 1)
            pool.memset(acc[:], 0.0).then_inc(zeroed, 1)
            pool.memset(ssq[:], 0.0).then_inc(zeroed, 1)

            pool.wait_ge(slots_zero, 64)
            with pool.Fori(0, NT // CH) as q:
                for r in range(CH):
                    t = q * CH + r
                    pool.wait_ge(scattered[r], 16 * TOPK * q)
                    pool.nop(nofuse=True)
                    pool.tensor_copy(cur_pos[r][:], at_col(pos, t)).then_inc(idx_copied, 1)
                    pool.dma_start(row[:, r, :], at(xn_tile, t)).then_inc(row_loaded[r], 16)
                for r in range(CH):
                    t = q * CH + r
                    pool.wait_ge(idx_copied, t + 1)
                    pool.wait_ge(row_loaded[r], 16 * (q + 1))
                    pool.nop(nofuse=True)
                    for k in range(TOPK):
                        pool.indirect_dma_start(out=slot_x, out_offset=bass.IndirectOffsetOnAxis(cur_pos[r][:, k:k + 1], 0),
                                                in_=row[:, r, :], in_offset=None).then_inc(scattered[r], 16)

            for r in range(2):
                pool.wait_ge(y_stored[r], 16 * NPAIR // 2)
            with pool.Fori(0, NT // 2) as q:
                for r in range(2):
                    t = q * 2 + r
                    pool.wait_ge(summed, TOPK * t - TOPK * r)
                    if r:
                        pool.wait_ge(summed, TOPK * 2 * q)
                    pool.nop(nofuse=True)
                    pool.tensor_copy(picked[r][:], at_col(pos, t)).then_inc(picked_ready, 1)
                    pool.wait_ge(picked_ready, t + 1)
                    pool.nop(nofuse=True)
                    for k in range(TOPK):
                        pool.indirect_dma_start(out=yk[r][:, k, :], out_offset=None, in_=slot_y,
                                                in_offset=bass.IndirectOffsetOnAxis(picked[r][:, k:k + 1], 0)).then_inc(gathered[r], 16)

            pool.wait_ge(rmsv_ready, 1)
            pool.tensor_tensor(rms[:], rmsv[:], mhalf2[:], ALU.pow).then_inc(rms_ready, 1)

        @block.scalar
        def _(act):
            def rows_T(g):
                act.wait_ge(xT_mm, g + 1)
                act.wait_ge(logits_mm, g)
                act.nop(nofuse=True)
                for k in range(KD):
                    act.copy(xh[:, k, bass.ds(g * SB, SB)], bank[k][:]).then_inc(xh_ready, 1)
                for k in range(KD):
                    act.copy(xf[:, k, :], bank[k][:]).then_inc(xf_ready, 1)

            rows_T(0)
            act.wait_ge(sraw_loaded, 80)
            act.copy(swh[:], sraw[:]).then_inc(swh_ready, 1)
            act.wait_ge(dve_const, 2)
            for h in range(NH):
                act.activation(tab[:, h, 0:P], dm0[:], ACT.Exp, scale=ns_all[:, h:h + 1]).then_inc(tables, 1)
                act.activation(tab[:, h, P:2 * P], mrow[:], ACT.Exp, scale=ns_all[:, h:h + 1]).then_inc(tables, 1)
            act.activation(tab[:, :, 2 * P], karg[:], ACT.Exp).then_inc(tab_ready, 1)
            act.activation(tab[:, :, 2 * P + 1], ns_all[:], ACT.Exp, scale=float(P)).then_inc(tab_ready, 1)

            def group(g, more):
                act.wait_ge(lc_ready, g + 1)
                act.activation(pr[:].rearrange("p c e -> p (c e)"), lc[:].rearrange("p c e -> p (c e)"), ACT.Exp).then_inc(pr_ready, 1)
                for ft in range(FT):
                    j = g * FT + ft
                    act.wait_ge(sgu_mm, j + 1)
                    act.activation(ssg[:], bank[GU[ft % 2][0]][:], ACT.Silu).then_inc(ssg_ready, 1)
                    act.wait_ge(sh_ready, j + 1)
                    if ft == 0:
                        act.wait_ge(down_mm, g)
                    act.copy(shh[:, ft, :], sh[:]).then_inc(shh_ready, 1)
                if more:
                    rows_T(g + 1)

            with act.Fori(0, NSB - 1) as g:
                group(g, True)
            group(NSB - 1, False)

            def split_high(h, par):
                act.wait_ge(raw_loaded, 64 * (h + 1))
                act.copy(wh[par][:, 0:WC], raw[:, 0:WC]).then_inc(wh_ready, 1)
                act.wait_ge(wos_ready, h + 1)
                act.copy(wh[par][:, WC:WC + D], wos[:]).then_inc(wh_ready, 1)

            def step(i, experts):
                m = 2 * (i - PLAIN * NSB)

                def turned(r):
                    act.wait_ge(xsT_mm, m + r + 1)
                    act.copy(xsT[:].rearrange("p j k m -> p (j k m)"), bank[6][:]).then_inc(xsT_ready, 1)

                def silu_pair(r):
                    act.wait_ge(gu_mm, m + r + 1)
                    g = bank[7][:, 0:4 * F].rearrange("p (j f) -> p j f", j=2)[:, :, 0:F]
                    act.activation(sg[:], g, ACT.Silu).then_inc(sg_ready, 1)

                def result(r):
                    act.wait_ge(y_mm, m + r + 1)
                    act.wait_ge(y_stored[r], 8 * m)
                    for half in range(2):
                        ins = act.copy(ys[r][:, :, half * P:(half + 1) * P], bank[7 - half][:, 0:2 * P].rearrange("p (j m) -> p j m", j=2))
                    ins.then_inc(ys_ready, 1)

                act.wait_ge(k_mm, i + 1)
                act.activation(kT[:], bank[0][:], ACT.Silu).then_inc(k_silu, 1)
                if experts:
                    turned(0)
                act.wait_ge(v_mm, i + 1)
                act.activation(vT[:], bank[1][:], ACT.Silu).then_inc(v_silu, 1)
                if experts:
                    silu_pair(0)
                act.wait_ge(q_mm, i + 1)
                act.activation(qT[:], bank[2][:], ACT.Silu).then_inc(q_silu, 1)
                act.wait_ge(vT_mm, i + 1)
                act.copy(vt[:], bank[4][:]).then_inc(vt_ready, 1)
                if experts:
                    result(0)
                act.wait_ge(g_mm, i + 1)
                act.wait_ge(og_ready, i)
                act.activation(tg[:], bank[0][:], ACT.Tanh, scale=0.5).then_inc(tanh_done, 1)
                if experts:
                    turned(1)
                    silu_pair(1)
                    result(1)
                act.wait_ge(o_mm, i + 1)
                act.wait_ge(ssq_added, i)
                act.activation(o2[:], bank[5][:], ACT.Square).then_inc(o2_ready, 1)
                act.wait_ge(og_ready, i + 1)
                act.copy(ogh[:], og[:]).then_inc(ogh_ready, 1)

            act.wait_ge(routed, 2)
            act.wait_ge(part_stored, 16 * NSB)
            act.wait_ge(zeroed, 4)
            split_high(0, 0)

            def head(experts):
                def run(h, par):
                    step(h * NSB, experts)
                    act.wait_ge(out_mm, KD * (h * NSB + 1))
                    split_high(h + 1, 1 - par)
                    with act.Fori(1, NSB) as b:
                        step(h * NSB + b, experts)
                return run

            heads(act, 0, PLAIN // 2, head(False))
            heads(act, PLAIN // 2, GATHER // 2, head(True))
            heads(act, GATHER // 2, NH // 2, head(False))

            act.wait_ge(acc_added, KD * (NSTEP + 1))
            with act.Fori(0, NSB) as b:
                act.wait_ge(accT_mm, b)
                act.nop(nofuse=True)
                for k in range(KD):
                    act.copy(accs[k][:], acc[:, k, bass.ds(b * SB, SB)]).then_inc(accs_ready, 1)

        @block.vector
        def _(dve):
            dve.memset(zeros[:], 0.0).then_inc(dve_const, 1)
            for ap, value in ((ones[:], 1.0), (ones_bf[:], 1.0), (mhalf[:], -0.5), (mhalf2[:], -0.5),
                              (zero_e[:], 0.0)):
                dve.memset(ap, value)
            dve.memset(macc[:], 0.0).then_inc(macc_ready, 1)
            dve.wait_ge(consts_loaded, 48)
            dve.wait_ge(pool_step, 7)
            dve.tensor_scalar(ns_all[:], slope_b[:], -1.0, None, ALU.mult).then_inc(route, 1)
            dve.tensor_scalar(dm0[:], dm[:], 0.0, None, ALU.max).then_inc(route, 1)
            dve.wait_ge(route, 2)
            dve.tensor_tensor(karg[:], kcol[:], ns_all[:], ALU.mult).then_inc(dve_const, 1)
            NCONST = 2

            def statistics(g, g2, u):
                dve.wait_ge(x_loaded[u], 16 * (g2 + 1))
                dve.wait_ge(xn_ready, CH * g)
                for c in range(CH):
                    dve.bn_stats(stat[:, c, :], xin[u][:, c, :]).then_inc(stats_done, 1)
                dve.wait_ge(stats_done, CH * (g + 1))
                dve.nop(nofuse=True)
                for c in range(CH):
                    dve.bn_aggr(mv[:, c, :], stat[:, c, :]).then_inc(aggr_done, 1)
                dve.wait_ge(aggr_done, CH * (g + 1))
                dve.tensor_scalar(ve[:], mv[:, :, 1], LN_EPS, None, ALU.add).then_inc(var_ready, 1)

            def rows_low(g):
                dve.wait_ge(xf_ready, KD * (g + 1))
                dve.nop(nofuse=True)
                for k in range(KD):
                    dve.tensor_tensor(xl[:, k, bass.ds(g * SB, SB)], bank[k][:],
                                      xh[:, k, bass.ds(g * SB, SB)].bitcast(F32), ALU.subtract).then_inc(xl_ready, 1)

            statistics(0, 0, 0)
            rows_low(0)
            dve.wait_ge(swh_ready, 1)
            dve.tensor_tensor(swl[:], sraw[:], swh[:].bitcast(F32), ALU.subtract).then_inc(swl_ready, 1)

            def group(g, g2, u, more):
                n = [0]

                def link(ins):
                    n[0] += 1
                    ins.then_inc(route, 1)
                    dve.wait_ge(route, NCONST + g * LINKS + n[0])

                def shared(ft):
                    j = g * FT + ft
                    dve.wait_ge(ssg_ready, j + 1)
                    dve.wait_ge(shl_ready, j)
                    dve.tensor_tensor(sh[:], ssg[:], bank[GU[ft % 2][1]][:], ALU.mult).then_inc(sh_ready, 1)

                def shared_low(ft):
                    j = g * FT + ft
                    dve.wait_ge(shh_ready, j + 1)
                    dve.tensor_tensor(shl[:, ft, :], sh[:], shh[:, ft, :].bitcast(F32), ALU.subtract).then_inc(shl_ready, 1)

                dve.wait_ge(logits_mm, g + 1)
                lg = bank[2][:, 0:CH * E].rearrange("p (c e) -> p c e", c=CH)
                link(dve.tensor_reduce(mx[:], lg, AX.X, ALU.max))
                dve.tensor_tensor(lc[:], lg, mx[:].unsqueeze(2).to_broadcast([P, CH, E]), ALU.subtract).then_inc(lc_ready, 1)
                link(dve.tensor_tensor(lgb[:], lg, per_chunk(rbias[:]), ALU.add))
                dve.nop(nofuse=True)
                for c in range(CH):
                    ins = dve.max(m8[:, c, :], lgb[:, c, :])
                    link(ins) if c == CH - 1 else None
                if more:
                    statistics(g + 1, g2 + (u + 1) // 2, 1 - u)
                shared(0)
                dve.nop(nofuse=True)
                for c in range(CH):
                    ins = dve.max_index(i8[:, c, :], m8[:, c, :], lgb[:, c, :])
                    link(ins) if c == CH - 1 else None
                link(dve.tensor_copy(idxf[:].rearrange("p (c k) -> p c k", c=CH), i8[:, :, 0:TOPK]))
                shared_low(0)
                ohg = oh[:, bass.ds(g * CH * TOPK, CH * TOPK), :]
                link(dve.tensor_tensor(ohg, iota_e[:].unsqueeze(1).to_broadcast([P, CH * TOPK, E]),
                                       idxf[:].unsqueeze(2).to_broadcast([P, CH * TOPK, E]), ALU.is_equal))
                shared(1)
                dve.nop(nofuse=True)
                with nc.allow_low_precision(reason="counts below 256 are exact"):
                    dve.tensor_reduce(mask[:], ohg.rearrange("p (c k) e -> p c e k", k=TOPK), AX.X, ALU.add).then_inc(mask_ready, 1)
                shared_low(1)
                dve.wait_ge(pr_ready, g + 1)
                link(dve.tensor_reduce(z[:], pr[:], AX.X, ALU.add))
                link(dve.reciprocal(zi[:], z[:]))
                prod4 = prod[:].rearrange("p (c k) e -> p c k e", k=TOPK)
                ohg4 = ohg.rearrange("p (c k) e -> p c k e", k=TOPK)
                link(dve.tensor_tensor(prod4, ohg4, pr[:].unsqueeze(2).to_broadcast([P, CH, TOPK, E]), ALU.mult))
                shared(2)
                link(dve.tensor_reduce(pk[:].rearrange("p c k -> p (c k)"), prod[:], AX.X, ALU.add))
                shared_low(2)
                link(dve.tensor_tensor(pz[:], pk[:], zi[:].unsqueeze(2).to_broadcast([P, CH, TOPK]), ALU.mult))
                link(dve.tensor_reduce(ps4[:], pz[:], AX.X, ALU.add))
                link(dve.reciprocal(pi4[:], ps4[:]))
                link(dve.tensor_tensor(wgt[:, bass.ds(g * CH, CH), :], pz[:], pi4[:].unsqueeze(2).to_broadcast([P, CH, TOPK]), ALU.mult))
                shared(3)
                shared_low(3)
                dve.wait_ge(rank_mm, g + 1)
                rk = bank[3][:, 0:CH * E].rearrange("p (c e) -> p c e", c=CH)
                link(dve.tensor_tensor(prod4, ohg4, rk.unsqueeze(2).to_broadcast([P, CH, TOPK, E]), ALU.mult))
                dve.nop(nofuse=True)
                link(dve.tensor_reduce(rank[:, bass.ds(g * CH * TOPK, CH * TOPK)], prod[:], AX.X, ALU.add))
                link(dve.tensor_reduce(mgrp[:], mask[:].rearrange("p c e -> p e c"), AX.X, ALU.add))
                dve.tensor_tensor(macc[:], macc[:], mgrp[:], ALU.add).then_inc(macc_ready, 1)
                assert n[0] == LINKS, n
                if more:
                    rows_low(g + 1)
                dve.wait_ge(down_mm, g + 1)
                dve.wait_ge(part_stored, 16 * g)
                for c in range(CH):
                    half = (c % 2) * D
                    dve.tensor_tensor(res4[:, c, :], xin[u][:, c, :], bank[6 + c // 2][:, half:half + D],
                                      ALU.add).then_inc(part_ready, 1)

            with dve.Fori(0, NSB // 2 - 1) as g2:
                for u in range(2):
                    group(g2 * 2 + u, g2, u, True)
            group(NSB - 2, NSB // 2 - 1, 0, True)
            group(NSB - 1, NSB // 2 - 1, 1, False)

            done = [NCONST + NSB * LINKS]

            def link(ins):
                done[0] += 1
                ins.then_inc(route, 1)
                dve.wait_ge(route, done[0])

            dve.wait_ge(tot_mm, 1)
            link(dve.tensor_scalar(tot_a[:], bank[2][:, 0:E], float(P - 1), None, ALU.add))
            link(dve.tensor_single_scalar(tot_s[:], tot_a[:], P.bit_length() - 1, ALU.logical_shift_right))
            link(dve.tensor_copy(cnt[:], tot_s[:]))
            link(dve.tensor_tensor_scan(incl[:], cnt[:], zero_e[:], 0.0, ALU.add, ALU.add))
            link(dve.tensor_tensor(base[:], incl[:], cnt[:], ALU.subtract))
            link(dve.tensor_scalar(base2[:], base[:], float(P), None, ALU.mult))
            for g in range(NSB):
                s = slice(g * CH * TOPK, (g + 1) * CH * TOPK)
                link(dve.tensor_tensor(prod[:], oh[:, s, :], base2[:].unsqueeze(1).to_broadcast([P, CH * TOPK, E]), ALU.mult))
                link(dve.tensor_reduce(posf[:, s], prod[:], AX.X, ALU.add))
            dve.tensor_tensor(pos[:].rearrange("p t k -> p (t k)"), posf[:], rank[:], ALU.add).then_inc(routed, 1)
            for j in range(2):
                link(dve.tensor_scalar(le[:, j, :], incl[:], tcol[:, j:j + 1], None, ALU.is_le))
            link(dve.tensor_reduce(ecol[:], le[:], AX.X, ALU.add))
            dve.tensor_scalar(ecl[:], ecol[:], float(E - 1), None, ALU.min).then_inc(ecl_ready, 1)
            dve.wait_ge(etab_mm, 1)
            dve.tensor_copy(etab[:], bank[3][0:1, 0:2 * P]).then_inc(routed, 1)

            def split_low(h, par):
                dve.wait_ge(raw_loaded, 64 * (h + 1))
                dve.tensor_scalar(wos[:], raw[:, WC:WC + D], raw[:, WC + D:WC + D + 1], 0.5,
                                  ALU.mult, ALU.mult).then_inc(wos_ready, 1)
                dve.wait_ge(wh_ready, 2 * (h + 1))
                dve.tensor_tensor(wl[par][:, 0:WC], raw[:, 0:WC], wh[par][:, 0:WC].bitcast(F32), ALU.subtract)
                dve.tensor_tensor(wl[par][:, WC:WC + D], wos[:], wh[par][:, WC:WC + D].bitcast(F32), ALU.subtract)

            def head_tables(h, par):
                dve.tensor_copy(hc[par][:], at_col(tab, h)).then_inc(w_ready, 1)

            def add_out(i, b_prev):
                for k in range(KD):
                    dve.wait_ge(out_mm, KD * i + k + 1)
                    dve.wait_ge(acc_added, KD * i + k)
                    a = acc[:, k, bass.ds(b_prev * SB, SB)]
                    dve.tensor_tensor(a, a, bank[3 + k][:], ALU.add).then_inc(acc_added, 1)

            def step(i, b, b_prev, par, experts, zero_count=None):
                m = 2 * (i - PLAIN * NSB)
                dkT = per_chunk(hc[par][:, 0:P])
                qd = per_chunk(hc[par][:, P:2 * P])
                kd, bd = hc[par][:, 2 * P:2 * P + 1], hc[par][:, 2 * P + 1:2 * P + 2]

                def gated(r):
                    dve.wait_ge(sg_ready, m + r + 1)
                    up = bank[7][:, 0:4 * F].rearrange("p (j f) -> p j f", j=2)[:, :, F:2 * F]
                    dve.tensor_tensor(he[:], sg[:].unsqueeze(2).to_broadcast([P, 2, 2, F]),
                                      up.unsqueeze(2).to_broadcast([P, 2, 2, F]), ALU.mult).then_inc(he_ready, 1)

                def gated_T(r):
                    dve.wait_ge(hT_mm, m + r + 1)
                    dve.tensor_copy(hT[:].rearrange("p j m -> p (j m)"), bank[6][:, 0:2 * P]).then_inc(hT_ready, 1)

                if zero_count is not None:
                    dve.wait_ge(state_step, 4 * i)
                    dve.memset(state[:, 0, :], 0.0).then_inc(state_zero, 1)
                if experts:
                    gated(0)
                    gated_T(0)
                dve.wait_ge(q_silu, i + 1)
                dve.tensor_tensor(chunks(qp[:]), chunks(qT[:]), qd, ALU.mult).then_inc(qp_ready, 1)
                dve.wait_ge(kT_mm, i + 1)
                dve.tensor_scalar(kp[:], bank[3][:], kd, None, ALU.mult).then_inc(kp_ready, 1)
                dve.wait_ge(s_mm, i + 1)
                dve.tensor_tensor(chunks(sm[:]), chunks(bank[1][:]), dkT, ALU.mult).then_inc(sm_ready, 1)
                if experts:
                    gated(1)
                dve.wait_ge(kv_mm, i + 1)
                if zero_count is not None:
                    dve.wait_ge(state_zero, zero_count)
                for c in range(CH - 1):
                    dve.wait_ge(state_step, 4 * i + c)
                    dve.scalar_tensor_tensor(state[:, c + 1, :], state[:, c, :], bd, chunks(bank[2][:])[:, c, :],
                                             ALU.mult, ALU.add).then_inc(state_step, 1)
                if experts:
                    gated_T(1)
                add_out(i, b_prev)
                dve.wait_ge(o_mm, i + 1)
                dve.wait_ge(state_step, 4 * i + CH - 1)
                dve.scalar_tensor_tensor(state[:, 0, :], state[:, CH - 1, :], bd, chunks(bank[2][:])[:, CH - 1, :],
                                         ALU.mult, ALU.add).then_inc(state_step, 1)
                dve.wait_ge(tanh_done, i + 1)
                dve.wait_ge(o2_ready, i + 1)
                dve.scalar_tensor_tensor(og[:], tg[:], 1.0, bank[5][:], ALU.add, ALU.mult).then_inc(og_ready, 1)
                dve.wait_ge(ssq_added, i)
                q = ssq[:, bass.ds(b * SB, SB)]
                dve.tensor_tensor(q, q, o2[:], ALU.add).then_inc(ssq_added, 1)
                dve.wait_ge(ogh_ready, i + 1)
                dve.tensor_tensor(ogl[:], og[:], ogh[:].bitcast(F32), ALU.subtract).then_inc(ogl_ready, 1)

            def combine(t, n, r):
                dve.wait_ge(summed, TOPK * t)
                dve.nop(nofuse=True)
                dve.tensor_copy(cols[:], at_col(wgt, t)).then_inc(cols_ready, 1)
                dve.wait_ge(cols_ready, t + 1)
                dve.wait_ge(xr_loaded[r], 16 * (n + 1))
                dve.wait_ge(gathered[r], 16 * TOPK * (n + 1))
                for k in range(TOPK):
                    dve.wait_ge(summed, TOPK * t + k)
                    dve.scalar_tensor_tensor(xr[r][:], yk[r][:, k, :], cols[:, k:k + 1], xr[r][:],
                                             ALU.mult, ALU.add).then_inc(summed, 1)

            dve.wait_ge(part_stored, 16 * NSB)
            dve.wait_ge(zeroed, 4)
            dve.wait_ge(tab_ready, 3)
            split_low(0, 0)
            head_tables(0, 0)
            dve.wait_ge(zeroed, 6)

            def head(experts, gather):
                def run(h, par):
                    t0 = (h - GATHER) * CH
                    n0 = (h - GATHER) * 2
                    step(h * NSB, 0, NSB - 1, par, experts, 2 * h + 1)
                    split_low(h + 1, 1 - par)
                    head_tables((h + 1) % NH, 1 - par)
                    for b in range(1, SB_PER_SEQ) if gather else ():
                        combine(t0 + b - 1, n0 + (b - 1) // 2, (b - 1) % 2)
                        step(h * NSB + b, b, b - 1, par, experts)
                    if not gather:
                        with dve.Fori(1, SB_PER_SEQ) as b:
                            step(h * NSB + b, b, b - 1, par, experts)
                    b = SB_PER_SEQ
                    if gather:
                        combine(t0 + CH - 1, n0 + 1, 1)
                    step(h * NSB + b, b, b - 1, par, experts, 2 * h + 2)
                    with dve.Fori(SB_PER_SEQ + 1, NSB) as b:
                        step(h * NSB + b, b, b - 1, par, experts)
                return run

            heads(dve, 0, PLAIN // 2, head(False, False))
            heads(dve, PLAIN // 2, GATHER // 2, head(True, False))
            heads(dve, GATHER // 2, NH // 2, head(False, True))
            add_out(NSTEP, NSB - 1)

            dve.wait_ge(rms_mm, 1)
            dve.tensor_scalar(rmsv[:], bank[0][:, 0:NT], 1.0 / (NH * HD), RMS_EPS, ALU.mult, ALU.add).then_inc(rmsv_ready, 1)
            dve.wait_ge(rms_ready, 1)
            for b in range(NSB):
                dve.wait_ge(accT_mm, b + 1)
                for c in range(CH):
                    t = b * CH + c
                    r = (t // 2) % 4
                    if c % 2 == 0:
                        dve.wait_ge(res_loaded[r], 16 * (t // 8 + 1))
                    half = (c % 2) * D
                    o = halves(res[r])[:, c % 2, :]
                    dve.scalar_tensor_tensor(o, bank[4 + 2 * (b % 2) + c // 2][:, half:half + D], rms[:, t:t + 1], o,
                                             ALU.mult, ALU.add).then_inc(final, 1)

        @block.tensor
        def _(pe):
            def rows_T(g, u):
                pe.wait_ge(xn_ready, CH * (g + 1))
                pe.wait_ge(xl_ready, KD * g)
                pe.wait_ge(sh_ready, FT * g)
                for k in range(KD):
                    for c in range(CH):
                        mm = pe.transpose(bank[k][:, c * P:(c + 1) * P], xn[u][:, c, k * P:(k + 1) * P], ident[:])
                mm.then_inc(xT_mm, 1)

            pe.wait_ge(pool_step, 9)
            pe.wait_ge(dve_const, 2)
            pe.wait_ge(consts_loaded, 48)
            rows_T(0, 0)

            def group(g, u, more):
                tok = bass.ds(g * SB, SB)
                pe.wait_ge(xf_ready, KD * (g + 1))
                pe.wait_ge(mask_ready, g)
                for c in range(CH):
                    for k in range(KD):
                        mm = pe.matmul(bank[2][:, c * E:(c + 1) * E], xf[:, k, c * P:(c + 1) * P], rw[:, k, :],
                                       start=(k == 0), stop=(k == KD - 1))
                mm.then_inc(logits_mm, 1)
                pe.wait_ge(swl_ready, 1)
                pe.wait_ge(xl_ready, KD * (g + 1))
                for ft in range(FT):
                    j = g * FT + ft
                    if ft >= 2:
                        pe.wait_ge(sh_ready, j - 1)
                    elif ft == 1:
                        pe.wait_ge(sh_ready, FT * g)
                    for i in range(2):
                        dst = bank[GU[ft % 2][i]][:]
                        for k in range(KD):
                            c0 = (i * KD + k) * 512 + ft * P
                            lh, ll = swh[:, c0:c0 + P], swl[:, c0:c0 + P]
                            pe.matmul(dst, lh, xh[:, k, tok], start=(k == 0), stop=False)
                            pe.matmul(dst, lh, xl[:, k, tok], start=False, stop=False)
                            mm = pe.matmul(dst, ll, xh[:, k, tok], start=False, stop=(k == KD - 1))
                    mm.then_inc(sgu_mm, 1)
                pe.wait_ge(mask_ready, g + 1)
                pe.wait_ge(macc_ready, g + 1)
                for c in range(CH):
                    o = bank[3][:, c * E:(c + 1) * E]
                    pe.matmul(o, upper[:], mask[:, c, :], start=True, stop=False)
                    for j in range(c):
                        pe.matmul(o, ones_bf[:], mask[:, j, :], start=False, stop=False)
                    mm = pe.matmul(o, ones_bf[:], macc[:], start=False, stop=True)
                mm.then_inc(rank_mm, 1)
                if more:
                    rows_T(g + 1, 1 - u)
                pe.wait_ge(shl_ready, FT * (g + 1))
                pe.wait_ge(part_ready, CH * g)
                for c in range(CH):
                    dst = bank[6 + c // 2][:, (c % 2) * D:(c % 2 + 1) * D]
                    for ft in range(FT):
                        c0 = 2 * KD * 512 + ft * D
                        rh, rl = swh[:, c0:c0 + D], swl[:, c0:c0 + D]
                        lh, ll = shh[:, ft, c * P:(c + 1) * P], shl[:, ft, c * P:(c + 1) * P]
                        pe.matmul(dst, lh, rh, start=(ft == 0), stop=False)
                        pe.matmul(dst, lh, rl, start=False, stop=False)
                        mm = pe.matmul(dst, ll, rh, start=False, stop=(ft == FT - 1))
                mm.then_inc(down_mm, 1)

            with pe.Fori(0, NSB // 2 - 1) as g2:
                for u in range(2):
                    group(g2 * 2 + u, u, True)
            group(NSB - 2, 0, True)
            group(NSB - 1, 1, False)
            pe.wait_ge(macc_ready, NSB + 1)
            pe.matmul(bank[2][:, 0:E], ones_bf[:], macc[:], start=True, stop=True).then_inc(tot_mm, 1)
            pe.wait_ge(ecl_ready, 1)
            for j in range(2):
                mm = pe.matmul(bank[3][0:1, j * P:(j + 1) * P], ecl[:, j:j + 1], ident[:], start=True, stop=True)
            mm.then_inc(etab_mm, 1)

            def project(dst, par, which, b):
                for k in range(KD):
                    cols_ = slice((k * 4 + which) * P, (k * 4 + which + 1) * P)
                    tok = bass.ds(b * SB, SB)
                    lh, ll = wh[par][:, cols_], wl[par][:, cols_]
                    rh, rl = xh[:, k, tok], xl[:, k, tok]
                    pe.matmul(dst, lh, rh, start=(k == 0), stop=False)
                    pe.matmul(dst, lh, rl, start=False, stop=False)
                    mm = pe.matmul(dst, ll, rh, start=False, stop=(k == KD - 1))
                return mm

            def project_out(i, par):
                pe.wait_ge(ogl_ready, i)
                for f in range(KD):
                    cols_ = slice(WC + f * P, WC + (f + 1) * P)
                    lh, ll = wh[par][:, cols_], wl[par][:, cols_]
                    dst = bank[3 + f][:]
                    pe.matmul(dst, lh, ogh[:], start=True, stop=False)
                    pe.matmul(dst, lh, ogl[:], start=False, stop=False)
                    pe.matmul(dst, ll, ogh[:], start=False, stop=True).then_inc(out_mm, 1)

            def step(i, b, par, par_prev, experts):
                ch = [slice(c * P, (c + 1) * P) for c in range(CH)]
                m = 2 * (i - PLAIN * NSB)

                def turn(r):
                    pe.wait_ge(pair_loaded[r], 24 * m + 48)
                    pe.wait_ge(ys_ready, m + r)
                    for j in range(2):
                        for k in range(KD):
                            o = (j * KD + k) * P
                            mm = pe.transpose(bank[6][:, o:o + P], xs[r][:, j, k * P:(k + 1) * P], ident[:])
                    mm.then_inc(xsT_mm, 1)

                def gate_up(r):
                    pe.wait_ge(xsT_ready, m + r + 1)
                    for j in range(2):
                        for k in range(KD):
                            mm = pe.matmul(bank[7][:, j * 2 * F:(j + 1) * 2 * F], xsT[:, j, k, :],
                                           we[r][:, j, k * 2 * F:(k + 1) * 2 * F], start=(k == 0), stop=(k == KD - 1))
                    mm.then_inc(gu_mm, 1)

                def turn_gated(r):
                    pe.wait_ge(he_ready, m + r + 1)
                    for j in range(2):
                        mm = pe.transpose(bank[6][:, j * P:(j + 1) * P], he[:, j, :, :].rearrange("p a f -> p (a f)"), ident[:])
                    mm.then_inc(hT_mm, 1)

                def down(r):
                    pe.wait_ge(hT_ready, m + r + 1)
                    for j in range(2):
                        for half in range(2):
                            ps = slice(half * F, (half + 1) * F)
                            mm = pe.matmul(bank[7 - half][:, j * P:(j + 1) * P], hT[ps, j, :], we[r][ps, j, 2 * KD * F:], start=True, stop=True)
                    mm.then_inc(y_mm, 1)

                pe.wait_ge(tanh_done, i)
                project(bank[0][:], par, 1, b).then_inc(k_mm, 1)
                if experts:
                    turn(0)
                pe.wait_ge(sm_ready, i)
                project(bank[1][:], par, 2, b).then_inc(v_mm, 1)
                if experts:
                    gate_up(0)
                pe.wait_ge(state_step, 4 * i)
                project(bank[2][:], par, 0, b).then_inc(q_mm, 1)
                if experts:
                    turn_gated(0)
                pe.wait_ge(k_silu, i + 1)
                pe.wait_ge(acc_added, KD * i)
                for c in range(CH):
                    mm = pe.transpose(bank[3][:, ch[c]], kT[:, ch[c]], ident[:])
                mm.then_inc(kT_mm, 1)
                pe.wait_ge(v_silu, i + 1)
                for c in range(CH):
                    mm = pe.transpose(bank[4][:, ch[c]], vT[:, ch[c]], ident[:])
                mm.then_inc(vT_mm, 1)
                if experts:
                    down(0)
                project(bank[0][:], par, 3, b).then_inc(g_mm, 1)
                if experts:
                    turn(1)
                pe.wait_ge(q_silu, i + 1)
                for c in range(CH):
                    mm = pe.matmul(bank[1][:, ch[c]], kT[:, ch[c]], qT[:, ch[c]], start=True, stop=True)
                mm.then_inc(s_mm, 1)
                if experts:
                    gate_up(1)
                pe.wait_ge(kp_ready, i + 1)
                pe.wait_ge(vt_ready, i + 1)
                for c in range(CH):
                    mm = pe.matmul(bank[2][:, ch[c]], kp[:, ch[c]], vt[:, ch[c]], start=True, stop=True)
                mm.then_inc(kv_mm, 1)
                if experts:
                    turn_gated(1)
                project_out(i, par_prev)
                if experts:
                    down(1)
                pe.wait_ge(sm_ready, i + 1)
                pe.wait_ge(qp_ready, i + 1)
                pe.wait_ge(state_step, 4 * i + CH - 1)
                pe.wait_ge(og_ready, i)
                for c in range(CH):
                    pe.matmul(bank[5][:, ch[c]], vt[:, ch[c]], sm[:, ch[c]], start=True, stop=False)
                    mm = pe.matmul(bank[5][:, ch[c]], state[:, c, :], qp[:, ch[c]], start=False, stop=True)
                mm.then_inc(o_mm, 1)

            def head(experts):
                def run(h, par):
                    pe.wait_ge(w_ready, h + 1)
                    step(h * NSB, 0, par, 1 - par, experts)
                    with pe.Fori(1, NSB) as b:
                        step(h * NSB + b, b, par, par, experts)
                return run

            pe.wait_ge(routed, 2)
            pe.wait_ge(zeroed, 4)
            heads(pe, 0, PLAIN // 2, head(False))
            heads(pe, PLAIN // 2, GATHER // 2, head(True))
            heads(pe, GATHER // 2, NH // 2, head(False))
            project_out(NSTEP, 1)

            pe.wait_ge(ssq_added, NSTEP)
            for t in range(NT):
                mm = pe.matmul(bank[0][:, t:t + 1], ssq[:, t * P:(t + 1) * P], ones[:], start=True, stop=True)
            mm.then_inc(rms_mm, 1)
            for b in range(NSB):
                pe.wait_ge(accs_ready, KD * (b + 1))
                if b >= 2:
                    pe.wait_ge(final, CH * (b - 1))
                for c in range(CH):
                    for k in range(KD):
                        o = (c % 2) * D + k * P
                        mm = pe.transpose(bank[4 + 2 * (b % 2) + c // 2][:, o:o + P], accs[k][:, c * P:(c + 1) * P], ident[:])
                mm.then_inc(accT_mm, 1)


def kernel(**inputs):
    import numpy as np
    import concourse.bacc as bacc
    from concourse.bass_utils import run_bass_kernel_spmd as run

    a = {k: np.asarray(v) for k, v in inputs.items()}
    feats = a["L0_attn_w_qkv"].reshape(NH, 3, HD, KD, P)
    gates = a["L0_attn_w_gate"].reshape(NH, HD, KD, P)
    wg = a["L0_ffn_wg"].reshape(E, KD, P, F)
    wu = a["L0_ffn_wu"].reshape(E, KD, P, F)
    arrays = {
        "x_rows": a["L0_attn_hidden_states"].reshape(T, D),
        "slope_row": a["L0_attn_slope_rate"].reshape(NH),
        "wqkv_in": feats.transpose(0, 4, 3, 1, 2).reshape(NH, P, KD, 3 * HD),
        "wgate_in": gates.transpose(0, 3, 2, 1),
        "wout_in": a["L0_attn_w_out"].reshape(D, NH, HD).transpose(1, 2, 0),
        "norm_in": a["L0_attn_norm_w"].reshape(NH, HD, 1),
        "router_in": a["L0_ffn_router_w"],
        "bias_in": a["L0_ffn_router_bias"],
        "wexp_in": np.concatenate([np.stack([wg, wu], axis=3).transpose(0, 2, 1, 3, 4).reshape(E, P, KD * 2 * F),
                                   a["L0_ffn_wd"].reshape(E, F, KD, P).transpose(0, 2, 1, 3).reshape(E, P, P)], axis=2),
        "swg_in": a["L0_ffn_swg"],
        "swu_in": a["L0_ffn_swu"],
        "swd_in": a["L0_ffn_swd"],
    }
    arrays = {k: np.ascontiguousarray(v) for k, v in arrays.items()}
    nc = bacc.Bacc("TRN2", target_bir_lowering=False, num_devices=1)
    args = [nc.dram_tensor(k, v.shape, mybir.dt.from_np(v.dtype), kind="ExternalInput").ap() for k, v in arrays.items()]
    args.append(nc.dram_tensor("out_rows", (T, D), F32, kind="ExternalOutput").ap())
    lightning_moe(nc, *args)
    r = run(nc, [arrays], core_ids=[0])
    return r.results[0]["out_rows"].reshape(B, N, D)
```

```python
from contextlib import ExitStack

import concourse.bass as bass
from concourse import mybir

F32 = mybir.dt.float32
F32R = mybir.dt.float32r
BF16 = mybir.dt.bfloat16
I32 = mybir.dt.int32
U32 = mybir.dt.uint32
ALU = mybir.AluOpType
ACT = mybir.ActivationFunctionType
AX = mybir.AxisListType

P = 128
B, N, D = 2, 2048, 256
T = B * N
KD = D // P
NH, HD = 16, 128
SB = 512
NSB = T // SB
CH = SB // P
SB_PER_SEQ = N // SB
NT = T // P
E, F, TOPK = 64, 64, 4
SLOT_TILES = T * TOPK // P + E
S, HS = 2, 256
FT = S * HS // P
LN_EPS = 1e-5
RMS_EPS = 1e-6
NSTEP = NH * NSB
SW = 2 * KD * 512 + FT * D
PLAIN, GATHER = 2, 8
RA, RB = 8, 8
RMS_PARTS = ((0, 8), (8, 28), (28, 32))
RING = 3
assert PLAIN == 2
NPAIR = SLOT_TILES // 2
assert NPAIR == 2 * (GATHER - PLAIN) * NSB and NT == CH * (NH - GATHER)
WE = KD * 2 * F
assert 2 * F == P
SHARED_COLS = (slice(0, 2 * KD * 512), slice(2 * KD * 512, SW))
RMS_BANK = (0, 5, 0)
TURN = ((6, 7), (1, 2))
GU = ((4, 5), (0, 1))
LINKS = 9
WC = KD * 4 * P
TAB = 2 * P + 2


def lightning_moe(nc, x, slope, wqkv, wgate, wout, norm_w, router_w, router_bias,
                  wexp, wdown, swg, swu, swd, out):
    xn_dram = nc.dram_tensor("xn_rows", [T, D], F32, kind="Internal").ap()
    slot_x = nc.dram_tensor("slot_x", [SLOT_TILES * P, D], F32, kind="Internal").ap()
    slot_y = nc.dram_tensor("slot_y", [SLOT_TILES * P, D], F32, kind="Internal").ap()
    tab_dram = nc.dram_tensor("decay_tables", [NH, P, TAB], F32, kind="Internal").ap()
    part = nc.dram_tensor("part", [T, D], F32, kind="Internal").ap()
    part2 = nc.dram_tensor("part2", [T, D], F32, kind="Internal").ap()

    top = ExitStack()
    with top:
        def sem(name):
            return top.enter_context(nc.semaphore(name))

        def sb_in(stack):
            return lambda name, shape, dt=F32: stack.enter_context(nc.sbuf_tensor(name, shape, dt))

        bank = [top.enter_context(nc.psum_tensor(f"bank{i}", [P, 512], F32)) for i in range(8)]
        keep = sb_in(top)
        with ExitStack() as st:
            res_b = sb_in(st)("res_b", [P, NT - RA, D])
        xh = keep("xh", [P, KD, T], F32R)
        xl = keep("xl", [P, KD, T], F32R)
        ident = keep("ident", [P, P])
        ones = keep("ones", [P, 1])
        pos = keep("pos", [P, NT, TOPK], U32)
        wgt = keep("wgt", [P, NT, TOPK])
        etab = keep("etab", [1, 2 * P], I32)
        raw = keep("raw", [P, WC + D + 1 + TAB])
        rms = keep("rms", [P, NT])
        rmsv = keep("rmsv", [P, NT])
        mhalf2 = keep("mhalf2", [P, NT])

        xs = [keep(f"xs{i}", [P, 2, D]) for i in range(2)]
        we = [keep(f"we{i}", [P, 2, WE]) for i in range(2)]
        wd = [keep(f"wd{i}", [P, D]) for i in range(2)]

        with ExitStack() as st:
            sb = sb_in(st)
            lc = sb("lc", [P, NT, E])
            prod = sb("prod", [P, CH * TOPK, E])
            oh = sb("oh", [P, CH * TOPK, E], BF16)
            idxf = sb("idxf", [P, NT * TOPK])
            rank = sb("rank", [P, NT * TOPK])
            posf = sb("posf", [P, CH * TOPK])
            iota_e = sb("iota_e", [P, E])
            base2 = sb("base2", [P, E])
            z = sb("z", [P, NT])
            zi = sb("zi", [P, NT])
            pk = sb("pk", [P, NT, TOPK])
            pz = sb("pz", [P, NT, TOPK])
            ps4 = sb("ps4", [P, NT])
            pi4 = sb("pi4", [P, NT])
            ecl = sb("ecl", [P, 2])
        with ExitStack() as st:
            sb = sb_in(st)
            xsT = sb("xsT", [P, 2, KD, P])
            sg = sb("sg", [P, 2 * P])
            hT = sb("hT", [P, P])
            ys = [sb(f"ys{i}", [P, 2, D]) for i in range(2)]
        yk = [keep(f"yk{i}", [P, TOPK, D]) for i in range(2)]
        xr = [keep(f"xr{i}", [P, D]) for i in range(2)]
        cols = keep("cols", [P, TOPK])
        picked = [keep(f"picked{i}", [P, TOPK], U32) for i in range(2)]
        res_a = keep("res_a", [P, RA, D])

        with ExitStack() as st:
            sb = sb_in(st)
            sraw = sb("sraw", [P, SW])
            dm = sb("dm", [P, P])
            swh = sb("swh", [P, SW], F32R)
            swl = sb("swl", [P, SW], F32R)
            xf = sb("xf", [P, KD, SB])
            tab = sb("tab", [P, NH, TAB])
            xin = [sb(f"xin{i}", [P, CH, D]) for i in range(RING)]
            xn = sb("xn", [P, CH, D])
            warm = sb("warm", [P, 1])
            zeros = sb("zeros", [P, 2 * D])
            rw = sb("rw", [P, KD, E])
            rbias = sb("rbias", [P, E])
            stat = sb("stat", [P, CH, 6])
            mv = sb("mv", [P, CH, 2])
            ve = sb("ve", [P, CH])
            rs = sb("rs", [P, CH])
            mhalf = sb("mhalf", [P, CH])
            upper = sb("upper", [P, P], BF16)
            ones_bf = sb("ones_bf", [P, P], BF16)
            lgb = sb("lgb", [P, CH, E])
            m8 = sb("m8", [P, CH, 8])
            i8 = sb("i8", [P, CH, 8], U32)
            mx = sb("mx", [P, CH])
            mask = sb("mask", [P, CH, E], BF16)
            mgrp = sb("mgrp", [P, E])
            macc = sb("macc", [P, E], BF16)
            tot_a = sb("tot_a", [P, E], I32)
            tot_s = sb("tot_s", [P, E], I32)
            cnt = sb("cnt", [P, E])
            incl = sb("incl", [P, E])
            base = sb("base", [P, E])
            zero_e = sb("zero_e", [P, E])
            tcol = sb("tcol", [P, 2])
            le = sb("le", [P, 2, E])
            ecol = sb("ecol", [P, 2])
            slope_b = sb("slope_b", [P, NH])
            ns_all = sb("ns_all", [P, NH])
            dm0 = sb("dm0", [P, P])
            mrow = sb("mrow", [P, P])
            kcol = sb("kcol", [P, NH])
            karg = sb("karg", [P, NH])
            ssg = (sb("ssg0", [P, SB])[:], xf[:, 0, :])
            sh = (sb("sh0", [P, SB])[:], xf[:, 1, :])
            shh = sb("shh", [P, FT, SB], F32R)
            shl = sb("shl", [P, FT, SB], F32R)
            res4 = sb("res4", [P, CH, D])

        wh0 = keep("wh0", [P, WC + D], F32R)
        wl0 = keep("wl0", [P, WC + D], F32R)
        wos = keep("wos", [P, D])
        hc0 = keep("hc0", [P, TAB])
        assert 2 * (WC + D) + D + TAB <= SW + P
        kT = keep("kT", [P, SB])
        kv = keep("kv", [P, CH, 2 * HD])
        qT = keep("qT", [P, SB])
        tg = keep("tg", [P, SB])
        kp = keep("kp", [P, SB])
        sm = keep("sm", [P, SB])
        qp = keep("qp", [P, SB])
        state = keep("state", [P, CH, HD])
        o2 = keep("o2", [P, SB])
        og = keep("og", [P, SB])
        ogh = keep("ogh", [P, SB], F32R)
        assert 2 * (WC + D) + D + TAB + 12 * SB <= 3 * SW + P
        ogl = keep("ogl", [P, SB], F32R)
        cur_pos = [keep(f"cur_pos{r}", [P, TOPK], U32) for r in range(CH)]
        hc1 = keep("hc1", [P, TAB])
        wh1 = keep("wh1", [P, WC + D], F32R)
        xc = [keep(f"xc{i}", [P, KD, SB], F32R) for i in range(2)]
        assert NH * TAB >= 2 * KD * SB + WC + D
        acc = keep("acc", [P, KD, T])
        ssq = keep("ssq", [P, T])
        wl1 = keep("wl1", [P, WC + D], F32R)
        wh, wl, hc = (wh0, wh1), (wl0, wl1), (hc0, hc1)

        consts_loaded = sem("consts_loaded")
        sraw_loaded = sem("sraw_loaded")
        sdown_loaded = sem("sdown_loaded")
        pool_step = sem("pool_step")
        dve_const = sem("dve_const")
        tables = sem("tables")
        tab_ready = sem("tab_ready")
        x_loaded = [sem(f"x_loaded{u}") for u in range(RING)]
        slots_zero = sem("slots_zero")
        stats_done = sem("stats_done")
        aggr_done = sem("aggr_done")
        var_ready = sem("var_ready")
        rstd_ready = sem("rstd_ready")
        xn_ready = sem("xn_ready")
        xn_stored = sem("xn_stored")
        xT_mm = sem("xT_mm")
        xf_ready = sem("xf_ready")
        xh_ready = sem("xh_ready")
        xl_ready = sem("xl_ready")
        logits_mm = sem("logits_mm")
        route = sem("route")
        lc_ready = sem("lc_ready")
        pr_ready = sem("pr_ready")
        tab_stored = sem("tab_stored")
        slope_loaded = sem("slope_loaded")
        counted = sem("counted")
        base_step = sem("base_step")
        side_step = sem("side_step")
        pos_ready = sem("pos_ready")
        wgt_ready = sem("wgt_ready")
        mask_ready = sem("mask_ready")
        rank_mm = sem("rank_mm")
        macc_ready = sem("macc_ready")
        tot_mm = sem("tot_mm")
        etab_mm = sem("etab_mm")
        ecl_ready = sem("ecl_ready")
        routed = sem("routed")
        swh_ready = sem("swh_ready")
        swl_ready = sem("swl_ready")
        sgu_mm = sem("sgu_mm")
        ssg_ready = sem("ssg_ready")
        sh_ready = sem("sh_ready")
        shh_ready = sem("shh_ready")
        shl_ready = sem("shl_ready")
        down_mm = sem("down_mm")
        part_ready = sem("part_ready")
        part_stored = sem("part_stored")
        raw_loaded = sem("raw_loaded")
        wos_ready = sem("wos_ready")
        wh_ready = sem("wh_ready")
        w_ready = sem("w_ready")
        zeroed = sem("zeroed")
        k_mm = sem("k_mm")
        v_mm = sem("v_mm")
        q_mm = sem("q_mm")
        kT_mm = sem("kT_mm")
        g_mm = sem("g_mm")
        s_mm = sem("s_mm")
        kv_mm = sem("kv_mm")
        out_mm = sem("out_mm")
        o_mm = sem("o_mm")
        k_silu = sem("k_silu")
        v_silu = sem("v_silu")
        q_silu = sem("q_silu")
        kT_ready = sem("kT_ready")
        xc_ready = sem("xc_ready")
        tanh_done = sem("tanh_done")
        o2_ready = sem("o2_ready")
        ogh_ready = sem("ogh_ready")
        ogl_ready = sem("ogl_ready")
        qp_ready = sem("qp_ready")
        kp_ready = sem("kp_ready")
        sm_ready = sem("sm_ready")
        state_step = sem("state_step")
        state_zero = sem("state_zero")
        acc_added = sem("acc_added")
        og_ready = sem("og_ready")
        ssq_added = sem("ssq_added")
        row_loaded = [sem(f"row_loaded{r}") for r in range(CH)]
        idx_copied = sem("idx_copied")
        scattered = [sem(f"scattered{r}") for r in range(CH)]
        pair_loaded = [sem(f"pair_loaded{r}") for r in range(2)]
        xsT_mm = sem("xsT_mm")
        xsT_ready = sem("xsT_ready")
        gu_mm = sem("gu_mm")
        sg_ready = sem("sg_ready")
        hT_ready = sem("hT_ready")
        y_mm = sem("y_mm")
        ys_ready = sem("ys_ready")
        y_stored = [sem(f"y_stored{r}") for r in range(2)]
        cols_ready = sem("cols_ready")
        xr_loaded = [sem(f"xr_loaded{r}") for r in range(2)]
        picked_ready = sem("picked_ready")
        gathered = [sem(f"gathered{r}") for r in range(2)]
        summed = sem("summed")
        part2_stored = [sem(f"part2_stored{r}") for r in range(2)]
        rms_mm = sem("rms_mm")
        rmsv_ready = sem("rmsv_ready")
        rms_ready = sem("rms_ready")
        accT_mm = sem("accT_mm")
        final = sem("final")
        res_loaded = sem("res_loaded")
        more_loaded = [sem(f"more_loaded{r}") for r in range((NT - RA) // RB)]
        out_stored = sem("out_stored")

        x_grp = x.rearrange("(g c p) d -> g p c d", c=CH, p=P)
        xn_grp = xn_dram.rearrange("(g c p) d -> g p c d", c=CH, p=P)
        part_grp = part.rearrange("(g c p) d -> g p c d", c=CH, p=P)
        xn_tile = xn_dram.rearrange("(t p) d -> t p d", p=P)
        part_tile = part.rearrange("(t p) d -> t p d", p=P)
        part2_tile = part2.rearrange("(t p) d -> t p d", p=P)
        part2_all = part2.rearrange("(t p) d -> p t d", p=P)
        out_grp = out.rearrange("(g c p) d -> g p c d", c=CH, p=P)
        slot_x_pair = slot_x.rearrange("(t c p) d -> t p c d", c=2, p=P)
        slot_y_pair = slot_y.rearrange("(t c p) d -> t p c d", c=2, p=P)
        zero_parts = slot_x.rearrange("(q p n r) d -> q p n (r d)", q=NSB, p=P, r=2)

        def at(ap, i):
            rest = " ".join("abc"[1:len(ap.shape) - 1])
            return ap[bass.ds(i, 1)].rearrange(f"o a {rest} -> (o a) {rest}")

        def at_col(tensor, i):
            return tensor[:, bass.ds(i, 1), :].rearrange("p o n -> p (o n)")

        def chunks(ap):
            return ap.rearrange("p (c m) -> p c m", c=CH)

        def per_chunk(ap):
            return ap.unsqueeze(1).to_broadcast([P, CH, ap.shape[-1]])

        def heads(eng, first_pair, last_pair, head):
            with eng.Fori(first_pair, last_pair) as hp:
                for par in range(2):
                    head(2 * hp + par, par)

        def first_phase_stored(eng):
            eng.wait_ge(part_stored, 16 * NSB)
            eng.wait_ge(xn_stored, 16 * NSB)
            eng.wait_ge(slots_zero, 16 * NSB)
            eng.wait_ge(tab_stored, 16)

        def last_rows(t, n):
            return res_a[:, t:t + n, :] if t < RA else res_b[:, t - RA:t - RA + n, :]

        block = top.enter_context(nc.Block())

        @block.sync
        def _(sp):
            sp.dma_start(slope_b[:], slope.partition_broadcast(P)).then_inc(slope_loaded, 16)
            sp.dma_start(xin[0][:], x_grp[0]).then_inc(x_loaded[0], 16)
            for dst, src in ((rw[:], router_w.rearrange("(k p) e -> p k e", p=P)),
                             (rbias[:], router_bias.partition_broadcast(P))):
                sp.dma_start(dst, src).then_inc(consts_loaded, 16)
            w = sraw[:, 0:2 * KD * 512].rearrange("p (i k s h) -> p i k s h", i=2, k=KD, s=S)
            for i, src in enumerate((swg, swu)):
                for s in range(S):
                    sp.dma_start(w[:, i, :, s, :], src[s].rearrange("(k p) h -> p k h", p=P)).then_inc(sraw_loaded, 16)
            sp.dma_start(sraw[:, 2 * KD * 512:].rearrange("p (t d) -> p t d", d=D),
                         swd.rearrange("s (t p) d -> p (s t) d", p=P)).then_inc(sdown_loaded, 16)
            for u in range(1, RING):
                sp.dma_start(xin[u][:], x_grp[u]).then_inc(x_loaded[u], 16)

            def store_rows(g):
                sp.wait_ge(xn_ready, CH * (g + 1))
                sp.dma_start(xn_grp[g], xn[:]).then_inc(xn_stored, 16)

            def group(g):
                if g < NSB - 1:
                    store_rows(g + 1)
                sp.wait_ge(part_ready, CH * (g + 1))
                if g < NSB - RING:
                    sp.dma_start(xin[g % RING][:], x_grp[g + RING]).then_inc(x_loaded[g % RING], 16)
                sp.dma_start(part_grp[g], res4[:]).then_inc(part_stored, 16)

            store_rows(0)
            sp.wait_ge(tab_ready, 3)
            sp.dma_start(tab_dram.rearrange("h p n -> p h n"), tab[:]).then_inc(tab_stored, 16)
            for g in range(NSB - 2):
                group(g)

            def load_head(h):
                w = raw[:, 0:WC].rearrange("p (k n) -> p k n", k=KD)
                sp.dma_start(w[:, :, 0:3 * HD], at(wqkv, h)).then_inc(raw_loaded, 16)
                sp.dma_start(w[:, :, 3 * HD:4 * HD], at(wgate, h)).then_inc(raw_loaded, 16)
                sp.dma_start(raw[:, WC:WC + D], at(wout, h)).then_inc(raw_loaded, 16)
                sp.dma_start(raw[:, WC + D:WC + D + 1], at(norm_w, h)).then_inc(raw_loaded, 16)
                sp.dma_start(raw[:, WC + D + 1:], at(tab_dram, h)).then_inc(raw_loaded, 16)

            def next_head(h):
                sp.wait_ge(w_ready, h + 1)
                load_head((h + 1) % NH)

            sp.wait_ge(tab_stored, 16)
            load_head(0)
            for g in range(NSB - 2, NSB):
                group(g)

            def load_rows_to_scatter(first, last):
                with sp.Fori(first, last) as q:
                    for r in range(CH):
                        sp.wait_ge(scattered[r], 16 * TOPK * q)
                        sp.dma_start(xs[r // 2][:, r % 2, :], at(xn_tile, q * CH + r)).then_inc(row_loaded[r], 16)

            sp.wait_ge(xn_stored, 16 * NSB)
            next_head(0)
            load_rows_to_scatter(0, NT // CH // 2)
            next_head(1)
            load_rows_to_scatter(NT // CH // 2, NT // CH)
            next_head(2)

            def load_rows(q, r):
                sp.dma_start(xs[r][:], at(slot_x_pair, q)).then_inc(pair_loaded[r], 16)

            def load_experts(q, r):
                for j in range(2):
                    e = sp.value_load(etab[0:1, bass.ds(q * 2 + j, 1)], min_val=0, max_val=E - 1)
                    sp.dma_start(we[r][:, j, :], at(wexp, e)).then_inc(pair_loaded[r], 16)
                    sp.dma_start(wd[r][j * F:(j + 1) * F, :], at(wdown, e)).then_inc(pair_loaded[r], 16)

            def expert_step(m, more):
                for r in range(2):
                    q = 2 * m + r
                    sp.wait_ge(y_mm, q + 1)
                    if more:
                        load_rows(q + 2, r)
                        load_experts(q + 2, r)
                    sp.wait_ge(ys_ready, q + 1)
                    sp.dma_start(at(slot_y_pair, q), ys[r][:]).then_inc(y_stored[r], 16)

            sp.wait_ge(routed, 1)
            for r in range(2):
                load_experts(r, r)
            for r in range(CH):
                sp.wait_ge(scattered[r], 16 * TOPK * NT // CH)
            for r in range(2):
                load_rows(r, r)

            def expert_head(h, par):
                with sp.Fori(0, NSB) as b:
                    expert_step((h - PLAIN) * NSB + b, True)
                next_head(h + 1)

            heads(sp, PLAIN // 2, GATHER // 2 - 1, expert_head)
            expert_head(GATHER - 2, 0)
            m = (GATHER - 1 - PLAIN) * NSB
            with sp.Fori(0, NSB - 1) as b:
                expert_step(m + b, True)
            expert_step(m + NSB - 1, False)
            for r in range(2):
                sp.wait_ge(y_stored[r], 16 * NPAIR // 2)

            def gather_head(h, par):
                next_head(h)
                t0 = (h - GATHER) * CH
                for c2 in range(2):
                    for r in range(2):
                        sp.wait_ge(part2_stored[r], 16 * ((h - GATHER) * 2 + c2))
                        sp.dma_start(xr[r][:], at(part_tile, t0 + 2 * c2 + r)).then_inc(xr_loaded[r], 16)
                    for r in range(2):
                        sp.wait_ge(summed, TOPK * (t0 + 2 * c2 + r + 1))
                        sp.dma_start(at(part2_tile, t0 + 2 * c2 + r), xr[r][:]).then_inc(part2_stored[r], 16)

            sp.wait_ge(part_stored, 16 * NSB)
            heads(sp, GATHER // 2, NH // 2, gather_head)

            for r in range(2):
                sp.wait_ge(part2_stored[r], 16 * NT // 2)

            sp.dma_start(res_a[:], part2_all[:, 0:RA, :]).then_inc(res_loaded, 16)
            sp.wait_ge(g_mm, NSTEP)
            sp.wait_ge(xc_ready, 2 * (NSTEP + 1))
            for r in range((NT - RA) // RB):
                t = RA + r * RB
                sp.dma_start(last_rows(t, RB), part2_all[:, t:t + RB, :]).then_inc(more_loaded[r], 16)
            for b in range(NSB):
                sp.wait_ge(final, CH * (b + 1))
                sp.dma_start(out_grp[b], last_rows(b * CH, CH)).then_inc(out_stored, 16)
            sp.wait_ge(out_stored, 16 * NSB)

        @block.gpsimd
        def _(pool):
            exact = dict(allow_small_or_imprecise_dtypes=True)
            pool.memset(ident[:], 0.0).then_inc(pool_step, 1)
            pool.memset(upper[:], 1.0).then_inc(pool_step, 1)
            pool.iota(dm[:], [[1, P]], base=0, channel_multiplier=-1, **exact).then_inc(pool_step, 1)
            pool.iota(mrow[:], [[1, P]], base=1, channel_multiplier=0, **exact).then_inc(pool_step, 1)
            pool.iota(kcol[:], [[0, NH]], base=P - 1, channel_multiplier=-1, **exact).then_inc(pool_step, 1)
            pool.iota(iota_e[:], [[1, E]], base=0, channel_multiplier=0, **exact).then_inc(pool_step, 1)
            pool.iota(tcol[:], [[P, 2]], base=0, channel_multiplier=1, **exact).then_inc(pool_step, 1)
            pool.wait_ge(pool_step, 7)
            pool.affine_select(out=ident[:], in_=ident[:], pattern=[[-1, P]], compare_op=ALU.not_equal, fill=1.0,
                               base=0, channel_multiplier=1).then_inc(pool_step, 1)
            pool.affine_select(out=upper[:], in_=upper[:], pattern=[[1, P]], compare_op=ALU.is_gt, fill=0.0,
                               base=0, channel_multiplier=-1).then_inc(pool_step, 1)
            pool.wait_ge(dve_const, 1)

            def deviations(g):
                pool.wait_ge(var_ready, g + 1)
                pool.tensor_tensor(rs[:], ve[:], mhalf[:], ALU.pow).then_inc(rstd_ready, 1)

            def normalise(g):
                deviations(g)
                pool.wait_ge(rstd_ready, g + 1)
                pool.wait_ge(xn_stored, 16 * g)
                pool.wait_ge(xT_mm, g)
                pool.nop(nofuse=True)
                for c in range(CH):
                    pool.tensor_scalar(xn[:, c, :], xin[g % RING][:, c, :], mv[:, c, 0:1], rs[:, c:c + 1],
                                       ALU.subtract, ALU.mult).then_inc(xn_ready, 1)

            deviations(0)
            pool.wait_ge(tables, 2)
            pool.affine_select(out=tab[:, :, 0:P], in_=tab[:, :, 0:P], pattern=[[0, NH], [1, P]], compare_op=ALU.is_ge,
                               fill=0.0, base=0, channel_multiplier=-1).then_inc(tab_ready, 1)
            for g in range(1, NSB):
                normalise(g)

            pool.wait_ge(k_mm, 1)
            pool.wait_ge(ecl_ready, 1)
            pool.wait_ge(pr_ready, 1)
            pool.memset(ogh[:].bitcast(F32), 0.0).then_inc(zeroed, 1)
            pool.memset(ogl[:].bitcast(F32), 0.0).then_inc(zeroed, 1)
            first_phase_stored(pool)

            def scatter_row(q, r):
                pool.wait_ge(pos_ready, q + 1)
                pool.wait_ge(scattered[r], 16 * TOPK * q)
                pool.nop(nofuse=True)
                pool.tensor_copy(cur_pos[r][:], at_col(pos, q * CH + r)).then_inc(idx_copied, 1)
                pool.wait_ge(idx_copied, q * CH + r + 1)
                pool.wait_ge(row_loaded[r], 16 * (q + 1))
                pool.nop(nofuse=True)
                for k in range(TOPK):
                    pool.indirect_dma_start(out=slot_x, out_offset=bass.IndirectOffsetOnAxis(cur_pos[r][:, k:k + 1], 0),
                                            in_=xs[r // 2][:, r % 2, :], in_offset=None).then_inc(scattered[r], 16)

            with pool.Fori(0, NT // CH) as q:
                for r in range(CH):
                    scatter_row(q, r)

            for r in range(2):
                pool.wait_ge(y_stored[r], 16 * NPAIR // 2)
            with pool.Fori(0, NT // 2) as q:
                for r in range(2):
                    t = q * 2 + r
                    pool.wait_ge(summed, TOPK * t - TOPK * r)
                    if r:
                        pool.wait_ge(summed, TOPK * 2 * q)
                    pool.nop(nofuse=True)
                    pool.tensor_copy(picked[r][:], at_col(pos, t)).then_inc(picked_ready, 1)
                    pool.wait_ge(picked_ready, t + 1)
                    pool.nop(nofuse=True)
                    for k in range(TOPK):
                        pool.indirect_dma_start(out=yk[r][:, k, :], out_offset=None, in_=slot_y,
                                                in_offset=bass.IndirectOffsetOnAxis(picked[r][:, k:k + 1], 0)).then_inc(gathered[r], 16)

            for j, (lo, hi) in enumerate(RMS_PARTS):
                pool.wait_ge(rmsv_ready, j + 1)
                pool.tensor_tensor(rms[:, lo:hi], rmsv[:, lo:hi], mhalf2[:, lo:hi], ALU.pow).then_inc(rms_ready, 1)

        @block.scalar
        def _(act):
            def rows_T(g):
                act.wait_ge(xT_mm, g + 1)
                act.wait_ge(shl_ready, FT * g)
                act.nop(nofuse=True)
                for k in range(KD):
                    act.copy(xh[:, k, bass.ds(g * SB, SB)], bank[k][:]).then_inc(xh_ready, 1)
                for k in range(KD):
                    act.copy(xf[:, k, :], bank[k][:]).then_inc(xf_ready, 1)

            act.wait_ge(dve_const, 3)
            act.activation(tab[:, :, P:2 * P], tab[:, :, P:2 * P], ACT.Exp).then_inc(tables, 1)
            act.activation(tab[:, :, 2 * P], karg[:], ACT.Exp).then_inc(tab_ready, 1)
            act.activation(tab[:, :, 2 * P + 1], ns_all[:], ACT.Exp, scale=float(P)).then_inc(tab_ready, 1)

            def split_shared(i):
                part_cols = SHARED_COLS[i]
                act.wait_ge((sraw_loaded, sdown_loaded)[i], (64, 16)[i])
                act.copy(swh[:, part_cols], sraw[:, part_cols]).then_inc(swh_ready, 1)

            split_shared(0)
            rows_T(0)
            act.wait_ge(dve_const, 4)
            act.activation(tab[:, :, 0:P], tab[:, :, 0:P], ACT.Exp).then_inc(tables, 1)
            split_shared(1)

            def group(g, more):
                def gate(ft):
                    act.wait_ge(sgu_mm, g * FT + ft + 1)
                    if ft == 0:
                        act.wait_ge(logits_mm, g + 1)
                    act.activation(ssg[ft % 2], bank[GU[ft % 2][0]][:], ACT.Silu).then_inc(ssg_ready, 1)

                def high(ft):
                    act.wait_ge(sh_ready, g * FT + ft + 1)
                    if ft == 0:
                        act.wait_ge(down_mm, 2 * g)
                    act.copy(shh[:, ft, :], sh[ft % 2]).then_inc(shh_ready, 1)

                act.activation(warm[:], ones[:], ACT.Silu)
                gate(0)
                high(0)
                gate(1)
                high(1)
                act.dma_start(at(zero_parts, g), zeros[:].unsqueeze(1).to_broadcast([P, SLOT_TILES // 2 // NSB, 2 * D])).then_inc(slots_zero, 16)
                gate(2)
                high(2)
                gate(3)
                high(3)
                if more:
                    rows_T(g + 1)

            act.wait_ge(dve_const, 5)
            with act.Fori(0, NSB - 1) as g:
                group(g, True)

            def split_high_in(h, par):
                act.wait_ge(raw_loaded, 80 * (h + 1))
                act.copy(wh[par][:, 0:WC], raw[:, 0:WC]).then_inc(wh_ready, 1)

            def split_high_out(h, par):
                act.wait_ge(wos_ready, h + 1)
                act.copy(wh[par][:, WC:WC + D], wos[:]).then_inc(wh_ready, 1)

            def load_tokens(low, b):
                src = (xh, xl)[low][:, :, bass.ds(b * SB, SB)]
                act.copy(xc[low][:], src).then_inc(xc_ready, 1)

            def step(i, b_next, experts, next_weights=()):
                m = 2 * (i - PLAIN * NSB)

                def turned(r):
                    act.wait_ge(xsT_mm, m + r + 1)
                    act.copy(xsT[:].rearrange("p j k m -> p (j k m)"), bank[6][:]).then_inc(xsT_ready, 1)

                def silu_pair(r):
                    act.wait_ge(gu_mm, m + r + 1)
                    act.activation(sg[F:2 * F, :], bank[7][0:F, 0:2 * P], ACT.Silu).then_inc(sg_ready, 1)

                def result(r):
                    act.wait_ge(y_mm, m + r + 1)
                    act.wait_ge(y_stored[r], 8 * m)
                    for j in range(2):
                        ins = act.copy(ys[r][:, j, :], bank[6 + j][:, 0:D])
                    ins.then_inc(ys_ready, 1)

                if experts:
                    turned(0)
                act.wait_ge(k_mm, i + 1)
                act.activation(kv[:, 0:2, :].rearrange("p c n -> p (c n)"), bank[0][:], ACT.Silu).then_inc(k_silu, 1)
                act.wait_ge(v_mm, i + 1)
                act.activation(kv[:, 2:4, :].rearrange("p c n -> p (c n)"), bank[1][:], ACT.Silu).then_inc(v_silu, 1)
                if experts:
                    silu_pair(0)
                act.wait_ge(q_mm, i + 1)
                act.activation(qT[:], bank[2][:], ACT.Silu).then_inc(q_silu, 1)
                act.wait_ge(kT_mm, i + 1)
                act.copy(kT[:], bank[3][:]).then_inc(kT_ready, 1)
                if experts:
                    result(0)
                act.wait_ge(v_mm, i + 1)
                load_tokens(0, b_next)
                if experts:
                    turned(1)
                act.wait_ge(g_mm, i + 1)
                act.wait_ge(og_ready, i)
                act.activation(tg[:], bank[0][:], ACT.Tanh, scale=0.5).then_inc(tanh_done, 1)
                if experts:
                    silu_pair(1)
                load_tokens(1, b_next)
                if experts:
                    result(1)
                if next_weights:
                    first_phase_stored(act)
                    split_high_in(*next_weights)
                act.wait_ge(o_mm, i + 1)
                act.wait_ge(ssq_added, i)
                act.activation(o2[:], bank[5][:], ACT.Square).then_inc(o2_ready, 1)
                if next_weights:
                    split_high_out(*next_weights)
                act.wait_ge(og_ready, i + 1)
                act.copy(ogh[:], og[:]).then_inc(ogh_ready, 1)

            split_high_in(0, 0)
            split_high_out(0, 0)
            group(NSB - 1, False)
            act.wait_ge(tab_stored, 16)
            act.wait_ge(xl_ready, KD)
            load_tokens(0, 0)
            load_tokens(1, 0)
            act.wait_ge(lc_ready, NSB)
            act.activation(lc[:].rearrange("p t e -> p (t e)"), lc[:].rearrange("p t e -> p (t e)"), ACT.Exp).then_inc(pr_ready, 1)

            def head(experts):
                def run(h, par):
                    step(h * NSB, 1, experts, (h + 1, 1 - par))
                    with act.Fori(1, NSB - 1) as b:
                        step(h * NSB + b, b + 1, experts)
                    step(h * NSB + NSB - 1, 0, experts)
                return run

            for h in range(PLAIN):
                head(False)(h, h % 2)
            act.wait_ge(side_step, 7 * NSB)
            assert 2 * KD * P + 3 * P + 4 * D <= NT * E
            heads(act, PLAIN // 2, GATHER // 2, head(True))
            heads(act, GATHER // 2, NH // 2, head(False))

        @block.vector
        def _(dve):
            for ap, value in ((mhalf[:], -0.5), (mhalf2[:], -0.5), (ones[:], 1.0), (ones_bf[:], 1.0), (zero_e[:], 0.0)):
                dve.memset(ap, value)
            dve.memset(macc[:], 0.0).then_inc(macc_ready, 1)
            dve.wait_ge(macc_ready, 1)
            dve.wait_ge(slope_loaded, 16)
            dve.wait_ge(pool_step, 7)
            dve.tensor_scalar(ns_all[:], slope_b[:], -1.0, None, ALU.mult).then_inc(route, 1)
            dve.tensor_scalar(dm0[:], dm[:], 0.0, None, ALU.max).then_inc(dve_const, 1)
            dve.wait_ge(route, 1)
            dve.tensor_tensor(karg[:], kcol[:], ns_all[:], ALU.mult).then_inc(dve_const, 1)
            NCONST = 1

            def decay_args(cols_, row):
                return dve.tensor_tensor(tab[:, :, cols_], row.unsqueeze(1).to_broadcast([P, NH, P]),
                                         ns_all[:].unsqueeze(2).to_broadcast([P, NH, P]), ALU.mult)

            decay_args(slice(P, 2 * P), mrow[:]).then_inc(dve_const, 1)

            def statistics(g, q, u):
                dve.wait_ge(x_loaded[u], 16 * (q + 1))
                dve.wait_ge(xn_ready, CH * g)
                for c in range(CH):
                    dve.bn_stats(stat[:, c, :], xin[u][:, c, :]).then_inc(stats_done, 1)
                dve.wait_ge(stats_done, CH * (g + 1))
                dve.nop(nofuse=True)
                for c in range(CH):
                    dve.bn_aggr(mv[:, c, :], stat[:, c, :]).then_inc(aggr_done, 1)
                dve.wait_ge(aggr_done, CH * (g + 1))
                dve.tensor_scalar(ve[:], mv[:, :, 1], LN_EPS, None, ALU.add).then_inc(var_ready, 1)

            def rows_low(g):
                dve.wait_ge(xf_ready, KD * (g + 1))
                dve.nop(nofuse=True)
                for k in range(KD):
                    dve.tensor_tensor(xl[:, k, bass.ds(g * SB, SB)], bank[k][:],
                                      xh[:, k, bass.ds(g * SB, SB)].bitcast(F32), ALU.subtract).then_inc(xl_ready, 1)

            def shared_rest(i):
                part_cols = SHARED_COLS[i]
                dve.wait_ge(swh_ready, i + 1)
                dve.tensor_tensor(swl[:, part_cols], sraw[:, part_cols], swh[:, part_cols].bitcast(F32), ALU.subtract).then_inc(swl_ready, 1)

            statistics(0, 0, 0)
            dve.wait_ge(rstd_ready, 1)
            dve.nop(nofuse=True)
            for c in range(CH):
                dve.tensor_scalar(xn[:, c, :], xin[0][:, c, :], mv[:, c, 0:1], rs[:, c:c + 1],
                                  ALU.subtract, ALU.mult).then_inc(xn_ready, 1)
            shared_rest(0)
            dve.wait_ge(dve_const, 3)
            decay_args(slice(0, P), dm0[:]).then_inc(dve_const, 1)
            rows_low(0)
            dve.memset(zeros[:], 0.0).then_inc(dve_const, 1)
            shared_rest(1)
            dve.wait_ge(consts_loaded, 32)

            def group(g, q, u, more):
                n = [0]

                def link(ins):
                    n[0] += 1
                    ins.then_inc(route, 1)
                    dve.wait_ge(route, NCONST + g * LINKS + n[0])

                def shared(ft):
                    j = g * FT + ft
                    dve.wait_ge(ssg_ready, j + 1)
                    if ft >= 2:
                        dve.wait_ge(shl_ready, j - 1)
                    dve.tensor_tensor(sh[ft % 2], ssg[ft % 2], bank[GU[ft % 2][1]][:], ALU.mult).then_inc(sh_ready, 1)

                def shared_low(ft):
                    j = g * FT + ft
                    dve.wait_ge(shh_ready, j + 1)
                    dve.tensor_tensor(shl[:, ft, :], sh[ft % 2], shh[:, ft, :].bitcast(F32), ALU.subtract).then_inc(shl_ready, 1)

                dve.wait_ge(logits_mm, g + 1)
                lg = bank[2][:, 0:CH * E].rearrange("p (c e) -> p c e", c=CH)
                link(dve.tensor_reduce(mx[:], lg, AX.X, ALU.max))
                dve.tensor_tensor(lc[:, bass.ds(g * CH, CH), :], lg, mx[:].unsqueeze(2).to_broadcast([P, CH, E]), ALU.subtract).then_inc(lc_ready, 1)
                link(dve.tensor_tensor(lgb[:], lg, per_chunk(rbias[:]), ALU.add))
                dve.nop(nofuse=True)
                for c in range(CH):
                    ins = dve.max(m8[:, c, :], lgb[:, c, :])
                    link(ins) if c == CH - 1 else None
                dve.nop(nofuse=True)
                for c in range(CH):
                    ins = dve.max_index(i8[:, c, :], m8[:, c, :], lgb[:, c, :])
                    link(ins) if c == CH - 1 else None
                idx = idxf[:, bass.ds(g * CH * TOPK, CH * TOPK)]
                link(dve.tensor_copy(idx.rearrange("p (c k) -> p c k", c=CH), i8[:, :, 0:TOPK]))
                shared(0)
                if more:
                    statistics(g + 1, q + (u + 1) // RING, (u + 1) % RING)
                shared(1)
                link(dve.tensor_tensor(oh[:], iota_e[:].unsqueeze(1).to_broadcast([P, CH * TOPK, E]),
                                       idx.unsqueeze(2).to_broadcast([P, CH * TOPK, E]), ALU.is_equal))
                shared_low(0)
                shared_low(1)
                shared(2)
                dve.nop(nofuse=True)
                with nc.allow_low_precision(reason="counts below 256 are exact"):
                    dve.tensor_reduce(mask[:], oh[:].rearrange("p (c k) e -> p c e k", k=TOPK), AX.X, ALU.add).then_inc(mask_ready, 1)
                shared_low(2)
                shared(3)
                shared_low(3)
                dve.wait_ge(rank_mm, g + 1)
                rk = bank[3][:, 0:CH * E].rearrange("p (c e) -> p c e", c=CH)
                oh4 = oh[:].rearrange("p (c k) e -> p c k e", k=TOPK)
                prod4 = prod[:].rearrange("p (c k) e -> p c k e", k=TOPK)
                link(dve.tensor_tensor(prod4, oh4, rk.unsqueeze(2).to_broadcast([P, CH, TOPK, E]), ALU.mult))
                dve.nop(nofuse=True)
                link(dve.tensor_reduce(rank[:, bass.ds(g * CH * TOPK, CH * TOPK)], prod[:], AX.X, ALU.add))
                link(dve.tensor_reduce(mgrp[:], mask[:].rearrange("p c e -> p e c"), AX.X, ALU.add))
                dve.tensor_tensor(macc[:], macc[:], mgrp[:], ALU.add).then_inc(macc_ready, 1)
                assert n[0] == LINKS, n
                if more:
                    rows_low(g + 1)
                dve.wait_ge(part_stored, 16 * g)
                for c in range(CH):
                    dve.wait_ge(down_mm, 2 * g + c // 2 + 1)
                    half = (c % 2) * D
                    dve.tensor_tensor(res4[:, c, :], xin[u][:, c, :], bank[6 + c // 2][:, half:half + D],
                                      ALU.add).then_inc(part_ready, 1)

            def scale_out(h):
                dve.wait_ge(raw_loaded, 80 * (h + 1))
                dve.tensor_scalar(wos[:], raw[:, WC:WC + D], raw[:, WC + D:WC + D + 1], 0.5,
                                  ALU.mult, ALU.mult).then_inc(wos_ready, 1)

            def split_low_in(h, par):
                dve.wait_ge(wh_ready, 2 * (h + 1))
                dve.tensor_tensor(wl[par][:, 0:WC], raw[:, 0:WC], wh[par][:, 0:WC].bitcast(F32), ALU.subtract)

            def split_low_out(h, par):
                dve.tensor_tensor(wl[par][:, WC:WC + D], wos[:], wh[par][:, WC:WC + D].bitcast(F32), ALU.subtract)
                dve.tensor_copy(hc[par][:], raw[:, WC + D + 1:]).then_inc(w_ready, 1)

            with dve.Fori(0, NSB // RING) as q:
                for u in range(RING):
                    group(q * RING + u, q, u, True)
            group(NSB - 2, NSB // RING, 0, True)
            scale_out(0)
            split_low_in(0, 0)
            split_low_out(0, 0)
            group(NSB - 1, NSB // RING, 1, False)

            done = [0]

            def link(ins):
                done[0] += 1
                ins.then_inc(base_step, 1)
                dve.wait_ge(base_step, done[0])

            dve.wait_ge(tot_mm, 1)
            dve.tensor_scalar(tot_a[:], bank[3][:, CH * E:CH * E + E], float(P - 1), None, ALU.add).then_inc(counted, 1)
            dve.wait_ge(counted, 1)
            link(dve.tensor_single_scalar(tot_s[:], tot_a[:], P.bit_length() - 1, ALU.logical_shift_right))
            link(dve.tensor_copy(cnt[:], tot_s[:]))
            link(dve.tensor_tensor_scan(incl[:], cnt[:], zero_e[:], 0.0, ALU.add, ALU.add))
            link(dve.tensor_tensor(base[:], incl[:], cnt[:], ALU.subtract))
            link(dve.tensor_scalar(base2[:], base[:], float(P), None, ALU.mult))
            for j in range(2):
                link(dve.tensor_scalar(le[:, j, :], incl[:], tcol[:, j:j + 1], None, ALU.is_le))
            link(dve.tensor_reduce(ecol[:], le[:], AX.X, ALU.add))
            dve.tensor_scalar(ecl[:], ecol[:], float(E - 1), None, ALU.min).then_inc(ecl_ready, 1)

            def side(n, ins):
                ins.then_inc(side_step, 1)
                dve.wait_ge(side_step, n)

            def one_hot(n, b):
                idx = idxf[:, bass.ds(b * CH * TOPK, CH * TOPK)]
                side(n + 1, dve.tensor_tensor(oh[:], iota_e[:].unsqueeze(1).to_broadcast([P, CH * TOPK, E]),
                                              idx.unsqueeze(2).to_broadcast([P, CH * TOPK, E]), ALU.is_equal))

            def choose(n, values):
                side(n + 2, dve.tensor_tensor(prod[:].rearrange("p (c k) e -> p c k e", k=TOPK),
                                              oh[:].rearrange("p (c k) e -> p c k e", k=TOPK), values, ALU.mult))

            def place_first(b):
                one_hot(3 * b, b)

            def place_next(b):
                choose(3 * b, base2[:].unsqueeze(1).unsqueeze(1).to_broadcast([P, CH, TOPK, E]))

            def place_last(b):
                side(3 * b + 3, dve.tensor_reduce(posf[:], prod[:], AX.X, ALU.add))
                dve.nop(nofuse=True)
                dve.tensor_tensor(pos[:, bass.ds(b * CH, CH), :].rearrange("p t k -> p (t k)"), posf[:],
                                  rank[:, bass.ds(b * CH * TOPK, CH * TOPK)], ALU.add).then_inc(pos_ready, 1)

            def weigh_first(b):
                one_hot(3 * NSB + 4 * b, b)

            def weigh_next(b):
                choose(3 * NSB + 4 * b, lc[:, bass.ds(b * CH, CH), :].unsqueeze(2).to_broadcast([P, CH, TOPK, E]))

            def weigh_last(b):
                dve.nop(nofuse=True)
                side(3 * NSB + 4 * b + 3, dve.tensor_reduce(pk[:, bass.ds(b * CH, CH), :].rearrange("p c k -> p (c k)"), prod[:], AX.X, ALU.add))
                dve.nop(nofuse=True)
                side(3 * NSB + 4 * b + 4, dve.tensor_reduce(z[:, bass.ds(b * CH, CH)], lc[:, bass.ds(b * CH, CH), :], AX.X, ALU.add))

            def weights():
                n = 7 * NSB
                side(n + 1, dve.reciprocal(zi[:], z[:]))
                side(n + 2, dve.tensor_tensor(pz[:], pk[:], zi[:].unsqueeze(2).to_broadcast([P, NT, TOPK]), ALU.mult))
                side(n + 3, dve.tensor_reduce(ps4[:], pz[:], AX.X, ALU.add))
                side(n + 4, dve.reciprocal(pi4[:], ps4[:]))
                dve.tensor_tensor(wgt[:], pz[:], pi4[:].unsqueeze(2).to_broadcast([P, NT, TOPK]), ALU.mult).then_inc(wgt_ready, 1)

            def add_out(i, b_prev, start=False):
                if start:
                    first_phase_stored(dve)
                for k in range(KD):
                    dve.wait_ge(out_mm, KD * i + k + 1)
                    dve.wait_ge(acc_added, KD * i + k)
                    a = acc[:, k, bass.ds(b_prev * SB, SB)]
                    if start:
                        dve.tensor_copy(a, bank[3 + k][:]).then_inc(acc_added, 1)
                    else:
                        dve.tensor_tensor(a, a, bank[3 + k][:], ALU.add).then_inc(acc_added, 1)

            def step(i, b, b_prev, par, experts, last=False, beside=(), next_weights=(), next_out=None, start=False):
                m = 2 * (i - PLAIN * NSB)
                dkT = per_chunk(hc[par][:, 0:P])
                qd = per_chunk(hc[par][:, P:2 * P])
                kd, bd = hc[par][:, 2 * P:2 * P + 1], hc[par][:, 2 * P + 1:2 * P + 2]

                def gated(r):
                    dve.wait_ge(sg_ready, m + r + 1)
                    for j in range(2):
                        dve.tensor_tensor(hT[j * F:(j + 1) * F, :], sg[F:2 * F, j * P:(j + 1) * P],
                                          bank[7][F:2 * F, j * P:(j + 1) * P], ALU.mult).then_inc(hT_ready, 1)

                if beside:
                    beside[0](b)
                if experts:
                    gated(0)
                dve.wait_ge(q_silu, i + 1)
                dve.tensor_tensor(chunks(qp[:]), chunks(qT[:]), qd, ALU.mult).then_inc(qp_ready, 1)
                dve.wait_ge(v_silu, i + 1)
                dve.tensor_scalar(chunks(kp[:]), kv[:, :, 0:HD], kd, None, ALU.mult).then_inc(kp_ready, 1)
                if beside:
                    beside[1](b)
                if next_weights:
                    split_low_in(*next_weights)
                if next_out is not None:
                    scale_out(next_out)
                dve.wait_ge(s_mm, i + 1)
                dve.tensor_tensor(chunks(sm[:]), chunks(bank[1][:]), dkT, ALU.mult).then_inc(sm_ready, 1)
                if experts:
                    gated(1)
                dve.wait_ge(kv_mm, i + 1)
                for c in range(CH - 1):
                    dve.wait_ge(state_step, 4 * i + c)
                    dve.scalar_tensor_tensor(state[:, c + 1, :], state[:, c, :], bd, chunks(bank[2][:])[:, c, :],
                                             ALU.mult, ALU.add).then_inc(state_step, 1)
                add_out(i, b_prev, start)
                if beside:
                    beside[2](b)
                if next_weights:
                    split_low_out(*next_weights)
                dve.wait_ge(o_mm, i + 1)
                dve.wait_ge(state_step, 4 * i + CH - 1)
                if last:
                    dve.memset(state[:, 0, :], 0.0).then_inc(state_step, 1)
                else:
                    dve.scalar_tensor_tensor(state[:, 0, :], state[:, CH - 1, :], bd, chunks(bank[2][:])[:, CH - 1, :],
                                             ALU.mult, ALU.add).then_inc(state_step, 1)
                dve.wait_ge(tanh_done, i + 1)
                dve.wait_ge(o2_ready, i + 1)
                dve.scalar_tensor_tensor(og[:], tg[:], 1.0, bank[5][:], ALU.add, ALU.mult).then_inc(og_ready, 1)
                dve.wait_ge(ssq_added, i)
                q = ssq[:, bass.ds(b * SB, SB)]
                if start:
                    dve.tensor_copy(q, o2[:]).then_inc(ssq_added, 1)
                else:
                    dve.tensor_tensor(q, q, o2[:], ALU.add).then_inc(ssq_added, 1)
                dve.wait_ge(ogh_ready, i + 1)
                dve.tensor_tensor(ogl[:], og[:], ogh[:].bitcast(F32), ALU.subtract).then_inc(ogl_ready, 1)

            def combine(t, n, r):
                dve.wait_ge(summed, TOPK * t)
                dve.nop(nofuse=True)
                dve.tensor_copy(cols[:], at_col(wgt, t)).then_inc(cols_ready, 1)
                dve.wait_ge(cols_ready, t + 1)
                dve.wait_ge(xr_loaded[r], 16 * (n + 1))
                dve.wait_ge(gathered[r], 16 * TOPK * (n + 1))
                for k in range(TOPK):
                    dve.wait_ge(summed, TOPK * t + k)
                    dve.scalar_tensor_tensor(xr[r][:], yk[r][:, k, :], cols[:, k:k + 1], xr[r][:],
                                             ALU.mult, ALU.add).then_inc(summed, 1)

            def head(experts, gather, beside=(), start=False):
                def run(h, par):
                    t0 = (h - GATHER) * CH
                    n0 = (h - GATHER) * 2
                    step(h * NSB, 0, NSB - 1, par, experts, False, beside, (), h + 1, start)
                    for b in range(1, SB_PER_SEQ) if gather else ():
                        combine(t0 + b - 1, n0 + (b - 1) // 2, (b - 1) % 2)
                        step(h * NSB + b, b, b - 1, par, experts, b == SB_PER_SEQ - 1)
                    if not gather:
                        with dve.Fori(1, SB_PER_SEQ - 1) as b:
                            step(h * NSB + b, b, b - 1, par, experts, False, beside, (), None, start)
                        b = SB_PER_SEQ - 1
                        step(h * NSB + b, b, b - 1, par, experts, True, beside, (), None, start)
                    b = SB_PER_SEQ
                    if gather:
                        combine(t0 + CH - 1, n0 + 1, 1)
                    step(h * NSB + b, b, b - 1, par, experts, False, beside, (h + 1, 1 - par), None, start)
                    with dve.Fori(SB_PER_SEQ + 1, NSB - 1) as b:
                        step(h * NSB + b, b, b - 1, par, experts, False, beside, (), None, start)
                    b = NSB - 1
                    step(h * NSB + b, b, b - 1, par, experts, True, beside, (), None, start)
                return run

            dve.wait_ge(k_mm, 1)
            dve.memset(state[:, 0, :], 0.0).then_inc(state_zero, 1)
            dve.wait_ge(state_zero, 1)
            head(False, False, (place_first, place_next, place_last), True)(0, 0)
            dve.wait_ge(etab_mm, 1)
            dve.tensor_copy(etab[:], bank[6][0:1, 0:2 * P]).then_inc(routed, 1)
            dve.wait_ge(pr_ready, 1)
            head(False, False, (weigh_first, weigh_next, weigh_last))(1, 1)
            weights()
            dve.wait_ge(wgt_ready, 1)
            heads(dve, PLAIN // 2, GATHER // 2, head(True, False))
            heads(dve, GATHER // 2, NH // 2, head(False, True))

            def mean_squares(j):
                lo, hi = RMS_PARTS[j]
                dve.wait_ge(rms_mm, j + 1)
                dve.tensor_scalar(rmsv[:, lo:hi], bank[RMS_BANK[j]][:, lo:hi], 1.0 / (NH * HD), RMS_EPS,
                                  ALU.mult, ALU.add).then_inc(rmsv_ready, 1)

            mean_squares(0)
            mean_squares(1)
            for b in range(NSB):
                if b == 1:
                    add_out(NSTEP, NSB - 1)
                    mean_squares(2)
                dve.wait_ge(accT_mm, b + 1)
                for c in range(CH):
                    t = b * CH + c
                    for j, (lo, hi) in enumerate(RMS_PARTS):
                        if t == lo:
                            dve.wait_ge(rms_ready, j + 1)
                    if t == 0:
                        dve.wait_ge(res_loaded, 16)
                    elif t >= RA and (t - RA) % RB == 0:
                        dve.wait_ge(more_loaded[(t - RA) // RB], 16)
                    o = last_rows(t, 1).rearrange("p o d -> p (o d)")
                    src = bank[TURN[b % 2][c // 2]][:, (c % 2) * D:(c % 2 + 1) * D]
                    dve.scalar_tensor_tensor(o, src, rms[:, t:t + 1], o, ALU.mult, ALU.add).then_inc(final, 1)

        @block.tensor
        def _(pe):
            def rows_T(g):
                pe.wait_ge(xn_ready, CH * (g + 1))
                pe.wait_ge(xl_ready, KD * g)
                pe.wait_ge(sh_ready, FT * g)
                for k in range(KD):
                    for c in range(CH):
                        mm = pe.transpose(bank[k][:, c * P:(c + 1) * P], xn[:, c, k * P:(k + 1) * P], ident[:])
                mm.then_inc(xT_mm, 1)

            pe.wait_ge(pool_step, 9)
            pe.wait_ge(macc_ready, 1)
            rows_T(0)
            pe.wait_ge(consts_loaded, 32)

            def group(g, more):
                tok = bass.ds(g * SB, SB)
                pe.wait_ge(xf_ready, KD * (g + 1))
                pe.wait_ge(mask_ready, g)
                for c in range(CH):
                    for k in range(KD):
                        mm = pe.matmul(bank[2][:, c * E:(c + 1) * E], xf[:, k, c * P:(c + 1) * P], rw[:, k, :],
                                       start=(k == 0), stop=(k == KD - 1))
                mm.then_inc(logits_mm, 1)
                pe.wait_ge(swl_ready, 1)
                pe.wait_ge(xl_ready, KD * (g + 1))
                for ft in range(FT):
                    j = g * FT + ft
                    if ft >= 2:
                        pe.wait_ge(sh_ready, j - 1)
                    elif ft == 1:
                        pe.wait_ge(sh_ready, FT * g)
                    for i in range(2):
                        dst = bank[GU[ft % 2][i]][:]
                        for k in range(KD):
                            c0 = (i * KD + k) * 512 + ft * P
                            lh, ll = swh[:, c0:c0 + P], swl[:, c0:c0 + P]
                            pe.matmul(dst, lh, xh[:, k, tok], start=(k == 0), stop=False)
                            pe.matmul(dst, lh, xl[:, k, tok], start=False, stop=False)
                            mm = pe.matmul(dst, ll, xh[:, k, tok], start=False, stop=(k == KD - 1))
                    mm.then_inc(sgu_mm, 1)
                pe.wait_ge(mask_ready, g + 1)
                pe.wait_ge(macc_ready, g + 1)
                for c in range(CH):
                    o = bank[3][:, c * E:(c + 1) * E]
                    pe.matmul(o, upper[:], mask[:, c, :], start=True, stop=False)
                    for j in range(c):
                        pe.matmul(o, ones_bf[:], mask[:, j, :], start=False, stop=False)
                    mm = pe.matmul(o, ones_bf[:], macc[:], start=False, stop=True)
                mm.then_inc(rank_mm, 1)
                def down(c, fts):
                    dst = bank[6 + c // 2][:, (c % 2) * D:(c % 2 + 1) * D]
                    for ft in fts:
                        c0 = 2 * KD * 512 + ft * D
                        rh, rl = swh[:, c0:c0 + D], swl[:, c0:c0 + D]
                        lh, ll = shh[:, ft, c * P:(c + 1) * P], shl[:, ft, c * P:(c + 1) * P]
                        pe.matmul(dst, lh, rh, start=(ft == 0), stop=False)
                        pe.matmul(dst, lh, rl, start=False, stop=False)
                        mm = pe.matmul(dst, ll, rh, start=False, stop=(ft == FT - 1))
                    return mm

                pe.wait_ge(swl_ready, 2)
                pe.wait_ge(part_ready, CH * g)
                pe.wait_ge(shl_ready, FT * g + FT - 1)
                for c in range(0, CH, 2):
                    down(c, range(FT - 1))
                if more:
                    rows_T(g + 1)
                pe.wait_ge(shl_ready, FT * (g + 1))
                for c in range(0, CH, 2):
                    down(c, range(FT - 1, FT))
                    down(c + 1, range(FT)).then_inc(down_mm, 1)

            with pe.Fori(0, NSB - 1) as g:
                group(g, True)
            group(NSB - 1, False)
            pe.wait_ge(macc_ready, NSB + 1)
            pe.matmul(bank[3][:, CH * E:CH * E + E], ones_bf[:], macc[:], start=True, stop=True).then_inc(tot_mm, 1)

            def project(dst, par, which, b):
                for k in range(KD):
                    cols_ = slice((k * 4 + which) * P, (k * 4 + which + 1) * P)
                    tok = bass.ds(b * SB, SB)
                    lh, ll = wh[par][:, cols_], wl[par][:, cols_]
                    rh, rl = xh[:, k, tok], xl[:, k, tok]
                    pe.matmul(dst, lh, rh, start=(k == 0), stop=False)
                    pe.matmul(dst, lh, rl, start=False, stop=False)
                    mm = pe.matmul(dst, ll, rh, start=False, stop=(k == KD - 1))
                return mm

            def project_kv(half, par):
                for c in range(2 * half, 2 * half + 2):
                    dst = bank[half][:, (c % 2) * 2 * HD:(c % 2 + 1) * 2 * HD]
                    for k in range(KD):
                        cols_ = slice((k * 4 + 1) * P, (k * 4 + 3) * P)
                        lh, ll = (xc[i][:, k, c * P:(c + 1) * P] for i in range(2))
                        rh, rl = wh[par][:, cols_], wl[par][:, cols_]
                        pe.matmul(dst, lh, rh, start=(k == 0), stop=False)
                        pe.matmul(dst, lh, rl, start=False, stop=False)
                        mm = pe.matmul(dst, ll, rh, start=False, stop=(k == KD - 1))
                return mm

            def project_out(i, par):
                pe.wait_ge(ogl_ready, i)
                pe.wait_ge(zeroed, 2)
                for f in range(KD):
                    cols_ = slice(WC + f * P, WC + (f + 1) * P)
                    lh, ll = wh[par][:, cols_], wl[par][:, cols_]
                    dst = bank[3 + f][:]
                    pe.matmul(dst, lh, ogh[:], start=True, stop=False)
                    pe.matmul(dst, lh, ogl[:], start=False, stop=False)
                    pe.matmul(dst, ll, ogh[:], start=False, stop=True).then_inc(out_mm, 1)

            def step(i, b, par, par_prev, experts, first=False, last=False):
                ch = [slice(c * P, (c + 1) * P) for c in range(CH)]
                m = 2 * (i - PLAIN * NSB)

                def turn(r):
                    pe.wait_ge(pair_loaded[r], 40 * m + 80)
                    pe.wait_ge(ys_ready, m + r)
                    for j in range(2):
                        for k in range(KD):
                            o = (j * KD + k) * P
                            mm = pe.transpose(bank[6][:, o:o + P], xs[r][:, j, k * P:(k + 1) * P], ident[:])
                    mm.then_inc(xsT_mm, 1)

                def gate_up(r):
                    pe.wait_ge(xsT_ready, m + r + 1)
                    for j in range(2):
                        for k in range(KD):
                            mm = pe.matmul(bank[7][:, j * P:(j + 1) * P], we[r][:, j, k * P:(k + 1) * P],
                                           xsT[:, j, k, :], start=(k == 0), stop=(k == KD - 1))
                    mm.then_inc(gu_mm, 1)

                def down(r):
                    pe.wait_ge(hT_ready, 2 * (m + r + 1))
                    for j in range(2):
                        ps = slice(j * F, (j + 1) * F)
                        mm = pe.matmul(bank[6 + j][:, 0:D], hT[ps, :], wd[r][ps, :], start=True, stop=True)
                    mm.then_inc(y_mm, 1)

                pe.wait_ge(xc_ready, 2 * i + 2)
                pe.wait_ge(tanh_done, i)
                project_kv(0, par).then_inc(k_mm, 1)
                if experts:
                    turn(0)
                pe.wait_ge(sm_ready, i)
                project_kv(1, par).then_inc(v_mm, 1)
                if experts:
                    gate_up(0)
                pe.wait_ge(state_step, 4 * i)
                project(bank[2][:], par, 0, b).then_inc(q_mm, 1)
                pe.wait_ge(k_silu, i + 1)
                pe.wait_ge(counted, 1)
                pe.wait_ge(acc_added, KD * i)
                for c in range(CH):
                    if c == CH // 2:
                        pe.wait_ge(v_silu, i + 1)
                    mm = pe.transpose(bank[3][:, ch[c]], kv[:, c, 0:HD], ident[:])
                mm.then_inc(kT_mm, 1)
                if experts:
                    down(0)
                project(bank[0][:], par, 3, b).then_inc(g_mm, 1)
                if experts:
                    turn(1)
                pe.wait_ge(q_silu, i + 1)
                pe.wait_ge(kT_ready, i + 1)
                for c in range(CH):
                    mm = pe.matmul(bank[1][:, ch[c]], kT[:, ch[c]], qT[:, ch[c]], start=True, stop=True)
                mm.then_inc(s_mm, 1)
                if experts:
                    gate_up(1)
                pe.wait_ge(kp_ready, i + 1)
                for c in range(CH - 1 if last else CH):
                    mm = pe.matmul(bank[2][:, ch[c]], kp[:, ch[c]], kv[:, c, HD:2 * HD], start=True, stop=True)
                mm.then_inc(kv_mm, 1)
                project_out(i, par_prev)
                if experts:
                    down(1)
                pe.wait_ge(sm_ready, i + 1)
                pe.wait_ge(qp_ready, i + 1)
                pe.wait_ge(og_ready, i)
                for c in range(CH):
                    pe.wait_ge(state_step, 4 * i + c)
                    empty = first and c == 0
                    mm = pe.matmul(bank[5][:, ch[c]], kv[:, c, HD:2 * HD], sm[:, ch[c]], start=True, stop=empty)
                    if not empty:
                        mm = pe.matmul(bank[5][:, ch[c]], state[:, c, :], qp[:, ch[c]], start=False, stop=True)
                mm.then_inc(o_mm, 1)

            def steps(h, par, par_prev, experts):
                pe.wait_ge(w_ready, h + 1)
                for b0 in range(0, NSB, SB_PER_SEQ):
                    step(h * NSB + b0, b0, par, par if b0 else par_prev, experts, first=True)
                    with pe.Fori(b0 + 1, b0 + SB_PER_SEQ - 1) as b:
                        step(h * NSB + b, b, par, par, experts)
                    step(h * NSB + b0 + SB_PER_SEQ - 1, b0 + SB_PER_SEQ - 1, par, par, experts, last=True)

            def head(experts):
                return lambda h, par: steps(h, par, 1 - par, experts)

            steps(0, 0, 0, False)
            pe.wait_ge(ecl_ready, 1)
            for j in range(2):
                mm = pe.matmul(bank[6][0:1, j * P:(j + 1) * P], ecl[:, j:j + 1], ident[:], start=True, stop=True)
            mm.then_inc(etab_mm, 1)
            for h in range(1, PLAIN):
                head(False)(h, h % 2)
            heads(pe, PLAIN // 2, GATHER // 2, head(True))
            heads(pe, GATHER // 2, NH // 2, head(False))

            def squares(j):
                for t in range(*RMS_PARTS[j]):
                    mm = pe.matmul(bank[RMS_BANK[j]][:, t:t + 1], ssq[:, t * P:(t + 1) * P], ones[:], start=True, stop=True)
                mm.then_inc(rms_mm, 1)

            def turn_back(b):
                if b >= 2:
                    pe.wait_ge(final, CH * (b - 1))
                for c in range(CH):
                    t = b * CH + c
                    for k in range(KD):
                        o = (c % 2) * D + k * P
                        mm = pe.transpose(bank[TURN[b % 2][c // 2]][:, o:o + P], acc[:, k, t * P:(t + 1) * P], ident[:])
                mm.then_inc(accT_mm, 1)

            pe.wait_ge(ssq_added, NSTEP - 1)
            pe.wait_ge(acc_added, KD * NSTEP)
            pe.wait_ge(tanh_done, NSTEP)
            squares(0)
            turn_back(0)
            pe.wait_ge(og_ready, NSTEP)
            squares(1)
            pe.wait_ge(sm_ready, NSTEP)
            pe.wait_ge(state_step, 4 * NSTEP)
            turn_back(1)
            project_out(NSTEP, 1)
            pe.wait_ge(ssq_added, NSTEP)
            pe.wait_ge(rmsv_ready, 1)
            squares(2)
            for b in range(2, NSB):
                if b == NSB - 1:
                    pe.wait_ge(acc_added, KD * (NSTEP + 1))
                turn_back(b)


def kernel(**inputs):
    import numpy as np
    import concourse.bacc as bacc
    from concourse.bass_utils import run_bass_kernel_spmd as run

    a = {k: np.asarray(v) for k, v in inputs.items()}
    feats = a["L0_attn_w_qkv"].reshape(NH, 3, HD, KD, P)
    gates = a["L0_attn_w_gate"].reshape(NH, HD, KD, P)
    wg = a["L0_ffn_wg"].reshape(E, KD, P, F)
    wu = a["L0_ffn_wu"].reshape(E, KD, P, F)
    arrays = {
        "x_rows": a["L0_attn_hidden_states"].reshape(T, D),
        "slope_row": a["L0_attn_slope_rate"].reshape(NH),
        "wqkv_in": feats.transpose(0, 4, 3, 1, 2).reshape(NH, P, KD, 3 * HD),
        "wgate_in": gates.transpose(0, 3, 2, 1),
        "wout_in": a["L0_attn_w_out"].reshape(D, NH, HD).transpose(1, 2, 0),
        "norm_in": a["L0_attn_norm_w"].reshape(NH, HD, 1),
        "router_in": a["L0_ffn_router_w"],
        "bias_in": a["L0_ffn_router_bias"],
        "wexp_in": np.stack([wg, wu], axis=3).transpose(0, 2, 1, 3, 4).reshape(E, P, WE),
        "wdown_in": a["L0_ffn_wd"],
        "swg_in": a["L0_ffn_swg"],
        "swu_in": a["L0_ffn_swu"],
        "swd_in": a["L0_ffn_swd"],
    }
    arrays = {k: np.ascontiguousarray(v) for k, v in arrays.items()}
    nc = bacc.Bacc("TRN2", target_bir_lowering=False, num_devices=1)
    args = [nc.dram_tensor(k, v.shape, mybir.dt.from_np(v.dtype), kind="ExternalInput").ap() for k, v in arrays.items()]
    args.append(nc.dram_tensor("out_rows", (T, D), F32, kind="ExternalOutput").ap())
    lightning_moe(nc, *args)
    r = run(nc, [arrays], core_ids=[0])
    return r.results[0]["out_rows"].reshape(B, N, D)
```
